# Optimizing a Trainium2 kernel written in Bass

```python
import numpy as np
import jax
import jax.numpy as jnp

def _softmax(x, axis=-1):
    return jax.nn.softmax(x, axis=axis)

def _gelu(x):
    return jax.nn.gelu(x, approximate=True)

def _silu(x):
    return jax.nn.silu(x)

def _sigmoid(x):
    return jax.nn.sigmoid(x)

def _layernorm(x, axis=-1, eps=1e-05):
    m = jnp.mean(x, axis=axis, keepdims=True)
    v = jnp.var(x, axis=axis, keepdims=True)
    return (x - m) / jnp.sqrt(v + eps)

def _scatter_add(tgt, idx, src, axis=0):
    return tgt.at[idx].add(src)

def _segment_sum(src, seg, n):
    return jax.ops.segment_sum(src, seg, n)
kernel_name = 'mk_adaln_d1_jaxref_r8_d61b3a'

def setup_inputs(seed: int=0):
    np.random.seed(seed)
    _w = jnp.asarray

    def _L0_attn_setup():
        import jax, jax.numpy as jnp
        import numpy as np
        INFTY_APPROX = 1e+30
        ROTARY_BASE = 10000.0
        ATTN_SCALE = 1.0 / 128.0

        def rope(x):
            T, D = (x.shape[-2], x.shape[-1])
            half = D // 2
            pos = jnp.arange(T, dtype=jnp.float32)[:, None]
            freqs = jnp.power(ROTARY_BASE, -jnp.arange(half, dtype=jnp.float32) / half)[None, :]
            rad = pos * freqs
            cos = jnp.cos(rad).astype(x.dtype)
            sin = jnp.sin(rad).astype(x.dtype)
            even, odd = jnp.split(x, 2, axis=-1)
            r_even = even * cos - odd * sin
            r_odd = even * sin + odd * cos
            return jnp.concatenate([r_even, r_odd], axis=-1)
        key = jax.random.key(seed)
        ks = jax.random.split(key, 5)
        B, T, M, H, D = (2, 256, 256, 16, 128)
        stddev = M ** (-0.5)
        return {'x': jax.random.normal(ks[0], (B, T, M), dtype=jnp.float32), 'wq': stddev * jax.random.normal(ks[1], (M, H, D), dtype=jnp.float32), 'wk': stddev * jax.random.normal(ks[2], (M, H, D), dtype=jnp.float32), 'wv': stddev * jax.random.normal(ks[3], (M, H, D), dtype=jnp.float32), 'wo': stddev * jax.random.normal(ks[4], (H, D, M), dtype=jnp.float32)}
    _L0_attn_in = _L0_attn_setup()

    def _L0_ffn_setup():
        import jax, jax.numpy as jnp
        import numpy as np
        B, S, H, E, K, I = (2, 128, 256, 32, 8, 96)
        key = jax.random.key(seed)
        ks = jax.random.split(key, 5)
        scaled = lambda k, shp, fan: jax.random.normal(k, shp, jnp.float32) * fan ** (-0.5)
        return {'hidden_states': jax.random.normal(ks[0], (B, S, H), jnp.float32), 'router_w': scaled(ks[1], (E, H), H), 'w_gate': scaled(ks[2], (E, H, I), H), 'w_up': scaled(ks[3], (E, H, I), H), 'w_down': scaled(ks[4], (E, I, H), I)}
    _L0_ffn_in = _L0_ffn_setup()
    _L0_c = _w((lambda *s: np.random.randn(*s).astype(np.float32) * 0.05)(4, 256))
    _L0_wmod = _w((lambda *s: np.random.randn(*s).astype(np.float32) * 0.05)(256, 6 * 256) * 256 ** (-0.5))
    _d = {'L0_attn_x': _L0_attn_in['x'], 'L0_attn_wq': _L0_attn_in['wq'], 'L0_attn_wk': _L0_attn_in['wk'], 'L0_attn_wv': _L0_attn_in['wv'], 'L0_attn_wo': _L0_attn_in['wo'], 'L0_ffn_router_w': _L0_ffn_in['router_w'], 'L0_ffn_w_gate': _L0_ffn_in['w_gate'], 'L0_ffn_w_up': _L0_ffn_in['w_up'], 'L0_ffn_w_down': _L0_ffn_in['w_down'], 'L0_c': _L0_c, 'L0_wmod': _L0_wmod}
    _x0 = _d['L0_attn_x']
    _d['L0_attn_x'] = jax.random.normal(jax.random.fold_in(jax.random.key(seed), 1), (4, 512, 256), dtype=_x0.dtype)
    del _x0
    return _d

def reference(L0_attn_x, L0_attn_wq, L0_attn_wk, L0_attn_wv, L0_attn_wo, L0_ffn_router_w, L0_ffn_w_gate, L0_ffn_w_up, L0_ffn_w_down, L0_c, L0_wmod):

    def _L0_attn_ref(x, wq, wk, wv, wo):
        import jax, jax.numpy as jnp
        import numpy as np
        INFTY_APPROX = 1e+30
        ROTARY_BASE = 10000.0
        ATTN_SCALE = 1.0 / 128.0

        def rope(x):
            T, D = (x.shape[-2], x.shape[-1])
            half = D // 2
            pos = jnp.arange(T, dtype=jnp.float32)[:, None]
            freqs = jnp.power(ROTARY_BASE, -jnp.arange(half, dtype=jnp.float32) / half)[None, :]
            rad = pos * freqs
            cos = jnp.cos(rad).astype(x.dtype)
            sin = jnp.sin(rad).astype(x.dtype)
            even, odd = jnp.split(x, 2, axis=-1)
            r_even = even * cos - odd * sin
            r_odd = even * sin + odd * cos
            return jnp.concatenate([r_even, r_odd], axis=-1)
        T = x.shape[1]
        q = jnp.einsum('bim,mhd->bhid', x, wq)
        k = jnp.einsum('bim,mhd->bhid', x, wk)
        v = jnp.einsum('bim,mhd->bhid', x, wv)
        q = rope(q)
        k = rope(k)
        mult = jnp.asarray(ATTN_SCALE ** 0.5, dtype=x.dtype)
        s = jnp.einsum('bhid,bhjd->bhij', q * mult, k * mult)
        i = jnp.arange(T)[:, None]
        j = jnp.arange(T)[None, :]
        mask = jnp.less(i, j).astype(s.dtype)[None, None, :, :]
        s = s - jnp.asarray(INFTY_APPROX, dtype=s.dtype) * mask
        p = jax.nn.softmax(s, axis=-1)
        o = jnp.einsum('bhij,bhjd->bhid', p, v)
        r = jnp.einsum('bhid,hdm->bim', o, wo)
        return r

    def _L0_ffn_ref(hidden_states, router_w, w_gate, w_up, w_down):
        import jax, jax.numpy as jnp
        import numpy as np
        B, S, H, E, K, I = (2, 128, 256, 32, 8, 96)
        Bq, Sq, Hd = hidden_states.shape
        x = hidden_states.reshape(-1, Hd)
        logits = x @ router_w.T
        probs = jax.nn.softmax(logits.astype(jnp.float32), axis=-1)
        rw, sel = jax.lax.top_k(probs, K)
        rw = rw / jnp.sum(rw, axis=-1, keepdims=True)
        rw = rw.astype(x.dtype)

        def body(acc, operand):
            e, wg, wu, wd = operand
            w_e = jnp.sum(jnp.where(sel == e, rw, jnp.zeros_like(rw)), axis=-1)
            h = jax.nn.silu(x @ wg) * (x @ wu)
            return (acc + h @ wd * w_e[:, None], None)
        acc0 = jnp.zeros_like(x)
        acc, _ = jax.lax.scan(body, acc0, (jnp.arange(E), w_gate, w_up, w_down))
        return acc.reshape(Bq, Sq, Hd)
    x = L0_attn_x
    mod = (_silu(L0_c) @ L0_wmod).reshape(L0_c.shape[0], 6, 1, -1)
    sa, ca, ga, sb, cb, gb = (mod[:, 0], mod[:, 1], mod[:, 2], mod[:, 3], mod[:, 4], mod[:, 5])
    ga = (2 * (ga >= 0) - 1) * jnp.maximum(jnp.abs(ga), 0.25)
    gb = (2 * (gb >= 0) - 1) * jnp.maximum(jnp.abs(gb), 0.25)
    h = _layernorm(x, axis=-1) * (1 + ca) + sa
    x = x + ga * _L0_attn_ref(h, L0_attn_wq, L0_attn_wk, L0_attn_wv, L0_attn_wo)
    h = _layernorm(x, axis=-1) * (1 + cb) + sb
    x = x + gb * _L0_ffn_ref(h, L0_ffn_router_w, L0_ffn_w_gate, L0_ffn_w_up, L0_ffn_w_down)
    return x

_drawn_inputs = setup_inputs


def setup_inputs(seed=0):
    import zlib

    import numpy as np

    out = dict(_drawn_inputs(seed))
    spreads = {}
    factors = {'L0_attn_wq': 7.871, 'L0_attn_wk': 7.798}
    for name, (base, spread) in spreads.items():
        noise = np.random.default_rng([zlib.crc32(name.encode()), seed]).standard_normal(out[name].shape)
        drawn = base * np.exp(spread * noise) if base else spread * noise
        out[name] = jnp.asarray(drawn.astype(out[name].dtype))
    for name, factor in factors.items():
        out[name] = (out[name] * factor).astype(out[name].dtype)
    return out
```

```python
import numpy as np
import concourse.bass as bass
from concourse import mybir
from contextlib import ExitStack

F32 = mybir.dt.float32
F32R = mybir.dt.float32r
BF16 = mybir.dt.bfloat16
ALU = mybir.AluOpType
ACT = mybir.ActivationFunctionType
AX = mybir.AxisListType

P = 128
B, T, M = 4, 512, 256
H, D = 16, 128
E, I, TOPK = 32, 96, 8
N = B * T
NT = N // P
TB = T // P
C = M // P
HEADS = B * H
PAIRS = H // 2
PER_PAIR = 2 * B
LOOPS = PAIRS - 1
FIRST = 2
CH = E * I // P
STEPS = CH * B
GROUP = 3
PER_GROUP = GROUP * B
GROUPS = CH // GROUP
FIRST_STEP = 3
EPS = 1e-5
KS = 3 * E
QB = [3, 2, 1, 0]
SA, CA, GA, SB_, CB, GB = range(6)
Y_CREDIT = 4
ADD_CREDIT = 1


def build(nc, x, xT, cT, wmod, rwT, rope, ident, identb, maskb, selb, wqk, wv, wo, wgu, wd, outT):
    ctx = ExitStack()
    with ctx:
        def sb(name, shape, dt=F32):
            return ctx.enter_context(nc.sbuf_tensor(name, shape, dt))

        def sem(name):
            return ctx.enter_context(nc.semaphore(name))

        accT = sb("accT", [P, C, N])
        hT_hi = sb("hT_hi", [P, C, N], F32R)
        hT_lo = sb("hT_lo", [P, C, N], F32R)
        xn = sb("xn", [P, NT, M])
        id_f = sb("id_f", [P, P])
        id_b = sb("id_b", [P, P], BF16)
        mask_b = sb("mask_b", [P, P], BF16)
        sel_b = sb("sel_b", [KS, E * I], BF16)
        rw_sb = sb("rw_sb", [P, C, E])
        c_sb = sb("c_sb", [P, C, B])
        c_silu = sb("c_silu", [P, C, B])
        mod = sb("mod", [P, 6 * C, B])
        gate = sb("gate", [P, 2, C, B])
        gsign = sb("gsign", [P, 2, C, B])
        gabs = sb("gabs", [P, 2, C, B])
        stats = sb("stats", [P, NT, 6])
        meanvar = sb("meanvar", [P, NT, 2])
        std = sb("std", [P, NT])
        rstd = sb("rstd", [P, NT])
        h_f = sb("h_f", [P, 4, T])
        wT_b = sb("wT_b", [KS, N], BF16)
        raw_gu = sb("raw_gu", [P, GROUP, C, 2, P])
        raw_d = sb("raw_d", [P, GROUP, M])

        att = ExitStack()

        def ab(name, shape, dt=F32):
            return att.enter_context(nc.sbuf_tensor(name, shape, dt))

        wmod_sb = ab("wmod_sb", [P, C, 6 * M])
        rope_sb = ab("rope_sb", [P, 4, T])
        raw_qk = ab("raw_qk", [P, 2, C, 2, P])
        raw_v = ab("raw_v", [P, C, 2 * D])
        raw_o = ab("raw_o", [P, 2, M])
        qk_hi = ab("qk_hi", [P, 2, C, 2, P], F32R)
        qk_lo = ab("qk_lo", [P, 2, C, 2, P], F32R)
        v_hi = ab("v_hi", [P, C, 2 * D], F32R)
        v_lo = ab("v_lo", [P, C, 2 * D], F32R)
        o_hi = ab("o_hi", [P, 2, M], F32R)
        o_lo = ab("o_lo", [P, 2, M], F32R)
        cosx = ab("cosx", [P, 2, T])
        sinx = ab("sinx", [P, 2, T])
        rot = ab("rot", [P, 2, 2, T])
        prob = ab("prob", [P, TB, T])
        probT = ab("probT", [P, 2, TB, T])
        vals = ab("vals", [P, 2, TB, 2 * D])
        ao_hi = ab("ao_hi", [P, 2, 2, T], F32R)
        ao_lo = ab("ao_lo", [P, 2, 2, T], F32R)
        negmax = ab("negmax", [P, 2, TB])
        rowsum = ab("rowsum", [P, 2, TB])
        rinv = ab("rinv", [P, 2, TB])
        att.close()

        h2_f = sb("h2_f", [P, C, N])
        logit = sb("logit", [P, NT, E])
        lmax = sb("lmax", [P, NT])
        ex = sb("ex", [P, NT, E])
        top = sb("top", [P, NT, TOPK])
        rest = sb("rest", [P, NT, E])
        wsum = sb("wsum", [P, NT])
        winv = sb("winv", [P, NT])
        w_f = sb("w_f", [P, NT, E])
        w_r = sb("w_r", [P, NT, E])
        w_b = sb("w_b", [P, NT, 3, E], BF16)
        gu_hi = sb("gu_hi", [P, GROUP, C, 2, P], F32R)
        gu_lo = sb("gu_lo", [P, GROUP, C, 2, P], F32R)
        d_hi = sb("d_hi", [P, GROUP, M], F32R)
        d_lo = sb("d_lo", [P, GROUP, M], F32R)
        sil = sb("sil", [P, 2, T])
        silw = sb("silw", [P, 2, T])
        hv = sb("hv", [P, 2, T])
        hv_hi = sb("hv_hi", [P, 2, T], F32R)
        hv_lo = sb("hv_lo", [P, 2, T], F32R)

        PS = ctx.enter_context(nc.psum_tensor("PS", [P, 8, T], F32))
        QKp = PS[:, 0:2, :]
        Sp = PS[:, 2:4, :]
        Tp = PS[:, 4, :]
        Op = PS[:, 5, :]
        Yp = PS[:, 6, :]
        Vp = PS[:, 7, :]

        ld_x = sem("ld_x")
        ld_c = sem("ld_c")
        ld_mod = sem("ld_mod")
        ld_const = sem("ld_const")
        ld_acc = sem("ld_acc")
        ld_qk = sem("ld_qk")
        ld_v = sem("ld_v")
        ld_o = sem("ld_o")
        ld_e = [sem(f"ld_e{j}") for j in range(GROUP)]
        stored = sem("stored")
        dve_step = sem("dve_step")
        silu_c = sem("silu_c")
        mod_done = sem("mod_done")
        mod_ready = sem("mod_ready")
        var_ready = sem("var_ready")
        std_ready = sem("std_ready")
        normed_x = sem("normed_x")
        ln_turned = sem("ln_turned")
        h_ready = sem("h_ready")
        h_hi = sem("h_hi")
        h_lo = sem("h_lo")
        whi_qk = sem("whi_qk")
        wlo_qk = sem("wlo_qk")
        whi_v = sem("whi_v")
        wlo_v = sem("wlo_v")
        whi_o = sem("whi_o")
        wlo_o = sem("wlo_o")
        qk_done = sem("qk_done")
        roped = sem("roped")
        rotated = sem("rotated")
        scored = sem("scored")
        maxed = sem("maxed")
        exped = sem("exped")
        inverted = sem("inverted")
        scaled = sem("scaled")
        turned = sem("turned")
        pt_out = sem("pt_out")
        v_done = sem("v_done")
        v_out = sem("v_out")
        pv_done = sem("pv_done")
        ao_hi_done = sem("ao_hi_done")
        ao_lo_done = sem("ao_lo_done")
        projected = sem("projected")
        added = sem("added")
        x1_turned = sem("x1_turned")
        logits_done = sem("logits_done")
        shifted = sem("shifted")
        ex_done = sem("ex_done")
        w_split = sem("w_split")
        wT_done = sem("wT_done")
        wT_ready = sem("wT_ready")
        whi_e = sem("whi_e")
        wlo_e = sem("wlo_e")
        g_done = sem("g_done")
        wb_done = sem("wb_done")
        u_done = sem("u_done")
        down_done = sem("down_done")
        sil_done = sem("sil_done")
        silw_done = sem("silw_done")
        hv_done = sem("hv_done")
        hv_hi_done = sem("hv_hi_done")
        hv_lo_done = sem("hv_lo_done")
        y_added = sem("y_added")

        block = ctx.enter_context(nc.Block())

        def reach(eng, s, v):
            if not isinstance(v, int) or v > 0:
                eng.wait_ge(s, v)

        def cols(b):
            return slice(b * T, (b + 1) * T)

        @block.sync
        def _(sp):
            sp.dma_start(xn[:, :, :], x).then_inc(ld_x, 16)
            sp.dma_start(c_sb[:, :, :], cT).then_inc(ld_c, 16)
            sp.dma_start(wmod_sb[:, :, :], wmod).then_inc(ld_mod, 16)
            sp.dma_start(id_f[:, :], ident).then_inc(ld_const, 16)
            for j in range(2):
                sp.dma_start(raw_qk[:, j], wqk[0, j]).then_inc(ld_qk, 16)
            sp.dma_start(raw_v[:, :, :], wv[0]).then_inc(ld_v, 16)
            sp.dma_start(raw_o[:, :, :], wo[0]).then_inc(ld_o, 16)
            sp.dma_start(rope_sb[:, :, :], rope).then_inc(ld_const, 16)
            sp.dma_start(id_b[:, :], identb).then_inc(ld_const, 16)
            sp.dma_start(mask_b[:, :], maskb).then_inc(ld_const, 16)
            sp.dma_start(accT[:, :, :], xT).then_inc(ld_acc, 16)
            sp.dma_start(rw_sb[:, :, :], rwT).then_inc(ld_const, 16)
            sp.dma_start(sel_b[:, :], selb).then_inc(ld_const, 16)
            for q in range(GROUP):
                sp.dma_start(raw_gu[:, q], wgu[q]).then_inc(ld_e[q], 16)
                sp.dma_start(raw_d[:, q], wd[q]).then_inc(ld_e[q], 16)
            with sp.Fori(0, LOOPS) as p:
                for j in range(2):
                    sp.wait_ge(wlo_qk, p * 2 + (j + 1))
                    sp.dma_start(raw_qk[:, j], wqk[p + 1, j]).then_inc(ld_qk, 16)
                sp.wait_ge(wlo_v, p + 1)
                sp.dma_start(raw_v[:, :, :], wv[p + 1]).then_inc(ld_v, 16)
                sp.wait_ge(wlo_o, p + 1)
                sp.dma_start(raw_o[:, :, :], wo[p + 1]).then_inc(ld_o, 16)
            with sp.Fori(0, GROUPS - 1) as g:
                for j in range(GROUP):
                    sp.wait_ge(wlo_e, g * GROUP + (j + 1))
                    sp.dma_start(raw_gu[:, j], wgu[(g + 1) * GROUP + j]).then_inc(ld_e[j], 16)
                    sp.dma_start(raw_d[:, j], wd[(g + 1) * GROUP + j]).then_inc(ld_e[j], 16)
            for b in range(B):
                sp.wait_ge(y_added, STEPS - B + b + 1)
                sp.dma_start(outT[:, :, cols(b)], accT[:, :, cols(b)]).then_inc(stored, 16)
            sp.wait_ge(stored, 16 * B)

        @block.tensor
        def _(pe):
            def mm3(out, hi, lo, rhs_hi, rhs_lo, k, n):
                nc.tensor.matmul(out, hi, rhs_hi, start=(k == 0), stop=False)
                nc.tensor.matmul(out, hi, rhs_lo, start=False, stop=False)
                return nc.tensor.matmul(out, lo, rhs_hi, start=False, stop=(k == n - 1))

            pe.wait_ge(ld_mod, 16)
            pe.wait_ge(silu_c, 1)
            for q in range(6 * C):
                for c in range(C):
                    last = nc.tensor.matmul(Op[:, q * B:(q + 1) * B], wmod_sb[:, c, q * P:(q + 1) * P],
                                            c_silu[:, c, :], start=(c == 0), stop=(c == C - 1))
            last.then_inc(mod_done, 1)

            def turn_h(r, i):
                b, c = divmod(i, C)
                reach(pe, normed_x, NT * r + (b + 1) * TB)
                reach(pe, h_ready, B * C * r + i - 3 if i >= 4 else 0)
                for t in range(TB):
                    last = nc.tensor.transpose(PS[:, 4 + i % 4 - (4 if r else 0), t * P:(t + 1) * P],
                                               xn[:, b * TB + t, c * P:(c + 1) * P], id_f[:, :])
                last.then_inc(ln_turned, 1)

            pe.wait_ge(ld_const, 16 * 6)
            pe.wait_ge(mod_ready, 1)
            for i in range(B * C):
                turn_h(0, i)

            def proj_qk(j, b, k):
                for c in range(C):
                    last = mm3(QKp[:, k], qk_hi[:, j, c, k], qk_lo[:, j, c, k],
                               hT_hi[:, c, cols(b)], hT_lo[:, c, cols(b)], c, C)
                last.then_inc(qk_done, 1)

            def proj_v(b, half):
                for t in range(2):
                    tok = slice(b * T + (2 * half + t) * P, b * T + (2 * half + t + 1) * P)
                    for c in range(C):
                        last = mm3(Vp[:, t * 2 * D:(t + 1) * 2 * D], hT_hi[:, c, tok], hT_lo[:, c, tok],
                                   v_hi[:, c, :], v_lo[:, c, :], c, C)
                last.then_inc(v_done, 1)

            def attend_v(par, j, upar):
                for kt in range(TB):
                    last = nc.tensor.matmul(Op[:, kt * P:T], vals[:, upar, kt, j * D:(j + 1) * D],
                                            probT[:, par, kt, kt * P:T], start=(kt == 0), stop=(kt == TB - 1))
                last.then_inc(pv_done, 1)

            def proj_o(upar, c):
                for j in range(2):
                    last = mm3(Yp, o_hi[:, j, c * P:(c + 1) * P], o_lo[:, j, c * P:(c + 1) * P],
                               ao_hi[:, upar, j, :], ao_lo[:, upar, j, :], j, 2)
                last.then_inc(projected, 1)

            def head(base, s, last_heads=False):
                m = base + s
                par = s % 2

                def score(o):
                    qb = QB[o]
                    w = (qb + 1) * P
                    if o == 0:
                        pe.wait_ge(rotated, m * 2 + 2)
                    reach(pe, exped, m * 4 + (o - 1) if not isinstance(m, int) or m * 4 + o - 1 > 0 else 0)
                    nc.tensor.matmul(Sp[:, o % 2, 0:w], rot[:, par, 0, qb * P:(qb + 1) * P],
                                     rot[:, par, 1, 0:w], start=True, stop=False)
                    nc.tensor.matmul(Sp[:, o % 2, qb * P:w], id_b[:, :], mask_b[:, :],
                                     start=False, stop=True).then_inc(scored, 1)

                def turn(o):
                    qb = QB[o]
                    pe.wait_ge(scaled, m * 4 + (o + 1))
                    reach(pe, pt_out, m * 4 + o)
                    for kt in range(qb + 1):
                        last = nc.tensor.transpose(Tp[:, kt * P:(kt + 1) * P],
                                                   prob[:, qb, kt * P:(kt + 1) * P], id_f[:, :])
                    last.then_inc(turned, 1)

                more = not last_heads or s < HEADS - 1
                nxt = (s + 1) % PER_PAIR
                nj, nb = nxt % 2, nxt // 2

                def qk(k):
                    if not more:
                        return
                    if k == 0 and nxt < 2:
                        pe.wait_ge(wlo_qk, base // 4 + ((s + 1) // 4 + nj + 1) if isinstance(base, int)
                                   else pair * 2 + ((s + 1) // PER_PAIR * 2 + nj + 1))
                    pe.wait_ge(roped, m * 2 + (k + 1))
                    proj_qk(nj, nb, k)

                pair = base_pair[0]
                score(0)
                score(1)
                qk(0)
                score(2)
                turn(0)
                qk(1)
                turn(1)
                score(3)
                if not isinstance(m, int) or m >= 1:
                    pe.wait_ge(pt_out, m * 4)
                    pe.wait_ge(v_out, m + (1 if s % 2 == 0 else 0) + 0 if s % 2 == 0 else m + 1)
                    reach(pe, ao_lo_done, m - 1 if not isinstance(m, int) or m > 1 else 0)
                    attend_v(1 - par, (s - 1) % 2, ((s - 1) // 2) % 2)
                turn(2)
                if not last_heads or s < HEADS - 2:
                    v = (s + 2) % PER_PAIR
                    if v == 0:
                        pe.wait_ge(wlo_v, (s + 2) // PER_PAIR + 1 if isinstance(base, int) else pair + ((s + 2) // PER_PAIR + 1))
                    pe.wait_ge(v_out, m + 2)
                    proj_v(v // 2, v % 2)
                if not isinstance(m, int) or m >= 2:
                    y_stage(m - 2, s - 2, pair)
                turn(3)

            def y_stage(y, s, pair):
                if s % PER_PAIR == 0:
                    pe.wait_ge(wlo_o, s // PER_PAIR + 1 if isinstance(y, int) else pair + (s // PER_PAIR + 1))
                pe.wait_ge(ao_lo_done, y + (2 - s % 2))
                pe.wait_ge(added, y + ADD_CREDIT)
                proj_o((s // 2) % 2, s % 2)

            base_pair = [0]
            pe.sem_inc(projected, Y_CREDIT)
            pe.wait_ge(h_lo, C)
            pe.wait_ge(wlo_qk, 1)
            proj_qk(0, 0, 0)
            proj_qk(0, 0, 1)
            pe.wait_ge(h_ready, B * C)
            pe.wait_ge(wlo_v, 1)
            for half in range(2):
                reach(pe, v_out, half)
                proj_v(0, half)
            pe.wait_ge(h_lo, B * C)
            for m in range(FIRST):
                head(0, m)
            with pe.Fori(0, LOOPS) as p:
                base_pair[0] = p
                for s in range(FIRST, FIRST + PER_PAIR):
                    head(p * PER_PAIR, s)
            base_pair[0] = 0
            for s in range(FIRST + LOOPS * PER_PAIR, HEADS):
                head(0, s, last_heads=True)
            pe.wait_ge(pt_out, 4 * HEADS)
            pe.wait_ge(ao_lo_done, HEADS - 1)
            attend_v(1, 1, 1)
            for y in range(HEADS - 2, HEADS):
                y_stage(y, y, 0)

            for b in range(B):
                pe.wait_ge(added, HEADS - (B - 1 - b) * 2 + ADD_CREDIT)
                if b == 3:
                    pe.wait_ge(ao_lo_done, HEADS)
                for t in range(TB):
                    i = b * TB + t
                    for c in range(C):
                        last = nc.tensor.transpose(PS[:, i // 2, (i % 2) * M + c * P:(i % 2) * M + (c + 1) * P],
                                                   accT[:, c, i * P:(i + 1) * P], id_f[:, :])
                last.then_inc(x1_turned, 1)
            pe.wait_ge(normed_x, 2 * NT)
            for i in range(B * C):
                turn_h(1, i)
            pe.wait_ge(h_ready, 2 * B * C)
            for i in range(NT):
                for c in range(C):
                    last = nc.tensor.matmul(PS[:, 4, i * E:(i + 1) * E], h2_f[:, c, i * P:(i + 1) * P],
                                            rw_sb[:, c, :], start=(c == 0), stop=(c == C - 1))
            last.then_inc(logits_done, 1)
            pe.wait_ge(w_split, 1)
            for i in range(NT):
                wps = PS[:, 5 + i // 8, :].bitcast(BF16)
                last = nc.tensor.transpose(wps[0:KS, (i % 8) * P:(i % 8 + 1) * P],
                                           w_b[:, i].rearrange("p s e -> p (s e)"), id_b[:, :])
            last.then_inc(wT_done, 1)

            def gate_up(j, b, k, t):
                bank = (0 if k == 0 else 2) + t % 2
                for c in range(C):
                    last = mm3(PS[:, bank], gu_hi[:, j, c, k], gu_lo[:, j, c, k],
                               hT_hi[:, c, cols(b)], hT_lo[:, c, cols(b)], c, C)
                return last

            def down(j, par):
                for c in range(C):
                    last = mm3(PS[:, 6 + c], d_hi[:, j, c * P:(c + 1) * P], d_lo[:, j, c * P:(c + 1) * P],
                               hv_hi[:, par], hv_lo[:, par], 0, 1)
                last.then_inc(down_done, 1)

            def step(base, s, grp):
                t = base + s
                j, b = (s // B) % GROUP, s % B
                if b == 0:
                    pe.wait_ge(wlo_e, grp + (s // B + 1) if isinstance(base, int) else grp * GROUP + (s // B + 1))
                reach(pe, sil_done, t - 1)
                gate_up(j, b, 0, s).then_inc(g_done, 1)
                reach(pe, silw_done, t - 1)
                if isinstance(base, int):
                    sel = sel_b[:, (s // B) * P:(s // B + 1) * P]
                else:
                    sel = sel_b[:, bass.ds(grp * (GROUP * P) + (s // B) * P, P)]
                nc.tensor.matmul(PS[:, 4 + s % 2], sel, wT_b[:, cols(b)],
                                 start=True, stop=True).then_inc(wb_done, 1)
                reach(pe, hv_done, t - 1)
                gate_up(j, b, 1, s).then_inc(u_done, 1)
                if not isinstance(t, int) or t >= 1:
                    pe.wait_ge(hv_lo_done, t)
                    reach(pe, y_added, t - 1)
                    down(((s - 1) // B) % GROUP, (s - 1) % 2)

            pe.wait_ge(wT_ready, 1)
            pe.wait_ge(h_lo, 2 * B * C)
            for t in range(FIRST_STEP):
                step(0, t, 0)
            with pe.Fori(0, GROUPS - 1) as g:
                for s in range(FIRST_STEP, FIRST_STEP + PER_GROUP):
                    step(g * PER_GROUP, s, g)
            for t in range(FIRST_STEP + (GROUPS - 1) * PER_GROUP, STEPS):
                step(0, t, 0)
            pe.wait_ge(hv_lo_done, STEPS)
            pe.wait_ge(y_added, STEPS - 1)
            down(GROUP - 1, 1)

        @block.scalar
        def _(act):
            act.wait_ge(ld_c, 16)
            nc.scalar.activation(c_silu[:, :, :], c_sb[:, :, :], ACT.Silu).then_inc(silu_c, 1)

            def split_qk(j, n, used):
                act.wait_ge(ld_qk, n)
                reach(act, qk_done, used)
                nc.scalar.activation(qk_hi[:, j], raw_qk[:, j], ACT.Copy).then_inc(whi_qk, 1)

            def split_v(n, used):
                act.wait_ge(ld_v, n)
                reach(act, v_done, used)
                nc.scalar.activation(v_hi[:, :, :], raw_v[:, :, :], ACT.Copy).then_inc(whi_v, 1)

            def split_o(n, used):
                act.wait_ge(ld_o, n)
                reach(act, projected, used)
                nc.scalar.activation(o_hi[:, :, :], raw_o[:, :, :], ACT.Copy).then_inc(whi_o, 1)

            split_qk(0, 32, 0)
            split_qk(1, 32, 0)
            split_v(16, 0)

            def h_high(r):
                for i in range(B * C):
                    b, c = divmod(i, C)
                    act.wait_ge(h_ready, B * C * r + i + 1)
                    src = h_f[:, i % 4] if r == 0 else h2_f[:, c, cols(b)]
                    nc.scalar.activation(hT_hi[:, c, cols(b)], src, ACT.Copy).then_inc(h_hi, 1)

            act.wait_ge(var_ready, 1)
            nc.scalar.activation(std[:, :], std[:, :], ACT.Sqrt).then_inc(std_ready, 1)
            h_high(0)

            def v_copy(v, s):
                act.wait_ge(v_done, v + 1)
                if not isinstance(v, int) or v >= 4:
                    act.wait_ge(pv_done, v - (2 + s % 2))
                nc.scalar.activation(vals[:, (s // 2) % 2, 2 * (s % 2):2 * (s % 2) + 2, :],
                                     Vp.rearrange("p (t d) -> p t d", t=2), ACT.Copy).then_inc(v_out, 1)

            def head(base, s, pair, last_heads=False):
                m = base + s
                par = s % 2

                def exp(o):
                    qb = QB[o]
                    w = (qb + 1) * P
                    act.wait_ge(maxed, m * 4 + (o + 1))
                    reach(act, turned, m * 4 + (o - 3) if not isinstance(m, int) or m > 0 else 0)
                    nc.scalar.activation(prob[:, qb, 0:w], Sp[:, o % 2, 0:w], ACT.Exp, bias=negmax[:, par, o:o + 1],
                                         accum_out=rowsum[:, par, o:o + 1]).then_inc(exped, 1)

                def pt_copy(o):
                    qb = QB[o]
                    act.wait_ge(turned, m * 4 + (o + 1))
                    reach(act, pv_done, m - 1 if not isinstance(m, int) or m > 1 else 0)
                    nc.scalar.activation(probT[:, par, 0:qb + 1, qb * P:(qb + 1) * P],
                                         Tp[:, 0:(qb + 1) * P].rearrange("p (k q) -> p k q", q=P),
                                         ACT.Copy).then_inc(pt_out, 1)

                if not last_heads:
                    nl = s // PER_PAIR
                    r = s % PER_PAIR
                    if r == 6:
                        split_v(pair * 16 + 16 * (nl + 2), pair * 8 + 8 * (nl + 1))
                        split_qk(0, pair * 32 + 32 * (nl + 2), pair * 16 + (16 * nl + 14))
                    if r == 7:
                        split_qk(1, pair * 32 + 32 * (nl + 2), pair * 16 + (16 * nl + 16))
                if s % PER_PAIR == 2:
                    nl = s // PER_PAIR
                    split_o(pair * 16 + 16 * (nl + 1), pair * 8 + (8 * nl + Y_CREDIT))
                exp(0)
                exp(1)
                pt_copy(0)
                exp(2)
                pt_copy(1)
                exp(3)
                if not isinstance(m, int) or m >= 1:
                    out_high(m - 1, s - 1)
                pt_copy(2)
                if not last_heads or s < HEADS - 2:
                    v_copy(m + 2, s + 2)
                pt_copy(3)

            def out_high(h, s):
                act.wait_ge(pv_done, h + 1)
                act.wait_ge(projected, h + (Y_CREDIT - 2 - s % 2))
                nc.scalar.activation(ao_hi[:, (s // 2) % 2, s % 2, :], Op, ACT.Copy).then_inc(ao_hi_done, 1)

            for half in range(2):
                v_copy(half, half)
            for m in range(FIRST):
                head(0, m, 0)
            with act.Fori(0, LOOPS) as p:
                for s in range(FIRST, FIRST + PER_PAIR):
                    head(p * PER_PAIR, s, p)
            for s in range(FIRST + LOOPS * PER_PAIR, HEADS):
                head(0, s, 0, last_heads=True)
            out_high(HEADS - 1, HEADS - 1)

            act.wait_ge(var_ready, 2)
            nc.scalar.activation(std[:, :], std[:, :], ACT.Sqrt).then_inc(std_ready, 1)
            h_high(1)
            act.wait_ge(shifted, 1)
            nc.scalar.activation(ex[:, :, :], logit[:, :, :], ACT.Exp).then_inc(ex_done, 1)

            def split_e(j, n, used):
                act.wait_ge(ld_e[j], n)
                reach(act, down_done, used)
                nc.scalar.activation(gu_hi[:, j], raw_gu[:, j], ACT.Copy)
                nc.scalar.activation(d_hi[:, j], raw_d[:, j], ACT.Copy).then_inc(whi_e, 1)

            def silu(t, s):
                act.wait_ge(g_done, t + 1)
                reach(act, silw_done, t - 1)
                nc.scalar.activation(sil[:, s % 2], PS[:, s % 2], ACT.Silu).then_inc(sil_done, 1)

            def high(t, s):
                act.wait_ge(hv_done, t + 1)
                reach(act, down_done, t - 1)
                nc.scalar.activation(hv_hi[:, s % 2], hv[:, s % 2], ACT.Copy).then_inc(hv_hi_done, 1)

            def step(base, s, grp, end=False):
                t = base + s
                silu(t, s)
                high(t, s)
                q = s // B + 2
                if s % B == 1 and not (end and q >= CH):
                    split_e(q % GROUP, grp * 32 + 32 * (q // GROUP + 1), base + (s - 1))

            split_e(0, 32, 0)
            split_e(1, 32, 0)
            for t in range(FIRST_STEP):
                step(0, t, 0)
            with act.Fori(0, GROUPS - 1) as g:
                for s in range(FIRST_STEP, FIRST_STEP + PER_GROUP):
                    step(g * PER_GROUP, s, g)
            for t in range(FIRST_STEP + (GROUPS - 1) * PER_GROUP, STEPS):
                step(0, t, 0, end=True)

        @block.vector
        def _(dve):
            chain = [0]

            def settle(ins):
                chain[0] += 1
                ins.then_inc(dve_step, 1)
                dve.wait_ge(dve_step, chain[0])

            def variances(src, r):
                for i in range(NT):
                    if r:
                        dve.wait_ge(x1_turned, i // TB + 1)
                    last = nc.vector.bn_stats(stats[:, i, :], src(i))
                settle(last)
                for i in range(NT):
                    last = nc.vector.bn_aggr(meanvar[:, i, :], stats[:, i, :])
                settle(last)
                nc.vector.tensor_scalar(std[:, :], meanvar[:, :, 1], EPS, None, ALU.add).then_inc(var_ready, 1)

            def norm(src, r):
                dve.wait_ge(std_ready, r + 1)
                settle(nc.vector.reciprocal(rstd[:, :], std[:, :]))
                for i in range(NT):
                    nc.vector.tensor_scalar(xn[:, i, :], src(i), meanvar[:, i, 0:1], rstd[:, i:i + 1],
                                            ALU.subtract, ALU.mult).then_inc(normed_x, 1)

            def modulate(r):
                sh, sc = (SA, CA) if r == 0 else (SB_, CB)
                for i in range(B * C):
                    b, c = divmod(i, C)
                    dve.wait_ge(ln_turned, B * C * r + i + 1)
                    if r == 0:
                        reach(dve, h_lo, i - 3)
                    dst = h_f[:, i % 4] if r == 0 else h2_f[:, c, cols(b)]
                    nc.vector.tensor_scalar(dst, PS[:, 4 + i % 4 - (4 if r else 0)], mod[:, sc * C + c, b:b + 1],
                                            mod[:, sh * C + c, b:b + 1], ALU.mult, ALU.add).then_inc(h_ready, 1)

            dve.wait_ge(ld_x, 16)
            variances(lambda i: xn[:, i, :], 0)
            dve.wait_ge(mod_done, 1)
            settle(nc.vector.tensor_copy(mod[:, :, :], Op[:, 0:6 * C * B].rearrange("p (q b) -> p q b", b=B)))
            for n, s in enumerate((CA, CB)):
                nc.vector.tensor_scalar(mod[:, s * C:(s + 1) * C, :], mod[:, s * C:(s + 1) * C, :], 1.0, None, ALU.add)
            for n, s in enumerate((GA, GB)):
                g = mod[:, s * C:(s + 1) * C, :]
                nc.vector.tensor_scalar(gsign[:, n], g, 0.0, 2.0, ALU.is_ge, ALU.mult)
                last = nc.vector.tensor_scalar(gabs[:, n], g, -1.0, None, ALU.mult)
            settle(last)
            settle(nc.vector.tensor_scalar(gsign[:, :], gsign[:, :], -1.0, None, ALU.add))
            for n, s in enumerate((GA, GB)):
                last = nc.vector.tensor_tensor(gabs[:, n], gabs[:, n], mod[:, s * C:(s + 1) * C, :], ALU.max)
            settle(last)
            settle(nc.vector.tensor_scalar(gabs[:, :], gabs[:, :], 0.25, None, ALU.max))
            nc.vector.tensor_tensor(gate[:, :], gabs[:, :], gsign[:, :], ALU.mult).then_inc(mod_ready, 1)
            dve.wait_ge(mod_ready, 1)
            norm(lambda i: xn[:, i, :], 0)
            modulate(0)

            def rope_mul(h, s, k):
                dve.wait_ge(qk_done, h * 2 + (k + 1))
                reach(dve, rotated, h * 2 + (k - 1) if not isinstance(h, int) or h > 0 else 0)
                nc.vector.tensor_tensor(cosx[:, k], QKp[:, k], rope_sb[:, k], ALU.mult)
                nc.vector.tensor_tensor(sinx[0:64, k], QKp[64:128, k], rope_sb[64:128, 2 + k], ALU.mult)
                nc.vector.tensor_tensor(sinx[64:128, k], QKp[0:64, k], rope_sb[0:64, 2 + k],
                                        ALU.mult).then_inc(roped, 1)

            def out_low(h, s):
                dve.wait_ge(ao_hi_done, h + 1)
                u, j = (s // 2) % 2, s % 2
                nc.vector.tensor_tensor(ao_lo[:, u, j, :], Op, ao_hi[:, u, j, :].bitcast(F32),
                                        ALU.subtract).then_inc(ao_lo_done, 1)

            def add_y(y, s):
                b, c = (s // 2) % B, s % 2
                dve.wait_ge(projected, y + (1 + Y_CREDIT))
                nc.vector.scalar_tensor_tensor(accT[:, c, cols(b)], Yp, gate[:, 0, c, b:b + 1], accT[:, c, cols(b)],
                                               ALU.mult, ALU.add).then_inc(added, 1)

            def head(base, s, last_heads=False):
                m = base + s
                par = s % 2

                def row_max(o):
                    w = (QB[o] + 1) * P
                    dve.wait_ge(scored, m * 4 + (o + 1))
                    nc.vector.tensor_reduce(negmax[:, par, o:o + 1], Sp[:, o % 2, 0:w], AX.X, ALU.max,
                                            negate=True).then_inc(maxed, 1)

                def scale(o):
                    qb = QB[o]
                    w = (qb + 1) * P
                    dve.wait_ge(exped, m * 4 + (o + 1))
                    nc.vector.reciprocal(rinv[:, par, o:o + 1], rowsum[:, par, o:o + 1]).then_inc(inverted, 1)
                    dve.wait_ge(inverted, m * 4 + (o + 1))
                    nc.vector.tensor_scalar(prob[:, qb, 0:w], prob[:, qb, 0:w], rinv[:, par, o:o + 1], None,
                                            ALU.mult).then_inc(scaled, 1)

                more = not last_heads or s < HEADS - 1
                row_max(0)
                row_max(1)
                scale(0)
                if more:
                    rope_mul(m + 1, s + 1, 0)
                scale(1)
                row_max(2)
                if more:
                    rope_mul(m + 1, s + 1, 1)
                row_max(3)
                scale(2)
                if not isinstance(m, int) or m >= 1:
                    out_low(m - 1, s - 1)
                scale(3)
                if not isinstance(m, int) or m >= 2:
                    add_y(m - 2, s - 2)

            dve.sem_inc(added, ADD_CREDIT)
            dve.wait_ge(ld_const, 16 * 6)
            dve.wait_ge(ld_acc, 16)
            rope_mul(0, 0, 0)
            rope_mul(0, 0, 1)
            for m in range(FIRST):
                head(0, m)
            with dve.Fori(0, LOOPS) as p:
                for s in range(FIRST, FIRST + PER_PAIR):
                    head(p * PER_PAIR, s)
            for s in range(FIRST + LOOPS * PER_PAIR, HEADS):
                head(0, s, last_heads=True)
            out_low(HEADS - 1, HEADS - 1)
            for y in range(HEADS - 2, HEADS):
                add_y(y, y)

            x1 = lambda i: PS[:, i // 2, (i % 2) * M:(i % 2 + 1) * M]
            variances(x1, 1)
            norm(x1, 1)
            modulate(1)

            dve.wait_ge(logits_done, 1)
            lg = PS[:, 4, :].rearrange("p (i e) -> p i e", e=E)
            settle(nc.vector.tensor_reduce(lmax[:, :], lg, AX.X, ALU.max))
            nc.vector.tensor_tensor(logit[:, :, :], lg, lmax[:, :].unsqueeze(2).to_broadcast([P, NT, E]),
                                    ALU.subtract).then_inc(shifted, 1)
            dve.wait_ge(ex_done, 1)
            for i in range(NT):
                last = nc.vector.max(top[:, i, :], ex[:, i, :])
            settle(last)
            for i in range(NT):
                last = nc.vector.match_replace(out=rest[:, i, :], in_to_replace=top[:, i, :],
                                               in_values=ex[:, i, :], imm_value=0.0)
            settle(last)
            settle(nc.vector.tensor_tensor(w_f[:, :, :], ex[:, :, :], rest[:, :, :], ALU.subtract))
            settle(nc.vector.tensor_reduce(wsum[:, :], w_f[:, :, :], AX.X, ALU.add))
            settle(nc.vector.reciprocal(winv[:, :], wsum[:, :]))
            settle(nc.vector.tensor_tensor(w_f[:, :, :], w_f[:, :, :],
                                           winv[:, :].unsqueeze(2).to_broadcast([P, NT, E]), ALU.mult))
            settle(nc.vector.tensor_copy(w_b[:, :, 0, :], w_f[:, :, :]))
            settle(nc.vector.tensor_tensor(w_r[:, :, :], w_f[:, :, :], w_b[:, :, 0, :], ALU.subtract))
            settle(nc.vector.tensor_copy(w_b[:, :, 1, :], w_r[:, :, :]))
            nc.vector.tensor_tensor(w_b[:, :, 2, :], w_r[:, :, :], w_b[:, :, 1, :], ALU.subtract).then_inc(w_split, 1)
            dve.wait_ge(wT_done, 1)
            wps = PS[0:KS, 5:7, :].bitcast(BF16)
            nc.vector.tensor_copy(wT_b[:, :].rearrange("k (a n) -> k a n", a=2), wps).then_inc(wT_ready, 1)

            def weigh(t, s):
                dve.wait_ge(sil_done, t + 1)
                dve.wait_ge(wb_done, t + 1)
                nc.vector.tensor_tensor(silw[:, s % 2], PS[:, 4 + s % 2], sil[:, s % 2], ALU.mult).then_inc(silw_done, 1)

            def times_up(t, s):
                dve.wait_ge(u_done, t + 1)
                dve.wait_ge(silw_done, t + 1)
                reach(dve, hv_lo_done, t - 1)
                nc.vector.tensor_tensor(hv[:, s % 2], PS[:, 2 + s % 2], silw[:, s % 2], ALU.mult).then_inc(hv_done, 1)

            def add_down(t, s):
                b = s % B
                dve.wait_ge(down_done, t + 1)
                for c in range(C):
                    last = nc.vector.scalar_tensor_tensor(accT[:, c, cols(b)], PS[:, 6 + c], gate[:, 1, c, b:b + 1],
                                                          accT[:, c, cols(b)], ALU.mult, ALU.add)
                last.then_inc(y_added, 1)

            def step(base, s):
                t = base + s
                weigh(t, s)
                times_up(t, s)
                if not isinstance(t, int) or t >= 1:
                    add_down(t - 1, s - 1)

            for t in range(FIRST_STEP):
                step(0, t)
            with dve.Fori(0, GROUPS - 1) as g:
                for s in range(FIRST_STEP, FIRST_STEP + PER_GROUP):
                    step(g * PER_GROUP, s)
            for t in range(FIRST_STEP + (GROUPS - 1) * PER_GROUP, STEPS):
                step(0, t)
            add_down(STEPS - 1, STEPS - 1)

        @block.gpsimd
        def _(pool):
            def low(dst, src, hi):
                return nc.gpsimd.tensor_tensor(dst, src, hi.bitcast(F32), ALU.subtract)

            def low_qk(j, n):
                pool.wait_ge(whi_qk, n)
                low(qk_lo[:, j], raw_qk[:, j], qk_hi[:, j]).then_inc(wlo_qk, 1)

            def low_v(n):
                pool.wait_ge(whi_v, n)
                low(v_lo[:, :, :], raw_v[:, :, :], v_hi[:, :, :]).then_inc(wlo_v, 1)

            def low_o(n):
                pool.wait_ge(whi_o, n)
                low(o_lo[:, :, :], raw_o[:, :, :], o_hi[:, :, :]).then_inc(wlo_o, 1)

            def h_low(r):
                for i in range(B * C):
                    b, c = divmod(i, C)
                    pool.wait_ge(h_hi, B * C * r + i + 1)
                    src = h_f[:, i % 4] if r == 0 else h2_f[:, c, cols(b)]
                    low(hT_lo[:, c, cols(b)], src, hT_hi[:, c, cols(b)]).then_inc(h_lo, 1)

            low_qk(0, 1)
            low_qk(1, 2)
            low_v(1)
            h_low(0)

            def rotate(h, s, k):
                pool.wait_ge(roped, h * 2 + (k + 1))
                reach(pool, scored, h * 4 - 4 if not isinstance(h, int) or h > 1 else 0)
                nc.gpsimd.tensor_tensor(rot[:, s % 2, k], cosx[:, k], sinx[:, k], ALU.add).then_inc(rotated, 1)

            def head(base, s, pair, last_heads=False):
                m = base + s
                nl = s // PER_PAIR
                r = s % PER_PAIR
                if not last_heads:
                    if r == 6:
                        low_v(pair + (nl + 2))
                        low_qk(0, pair * 2 + (2 * nl + 3))
                    if r == 7:
                        low_qk(1, pair * 2 + (2 * nl + 4))
                if r == 2:
                    low_o(pair + (nl + 1))
                if not last_heads or s < HEADS - 1:
                    rotate(m + 1, s + 1, 0)
                    rotate(m + 1, s + 1, 1)

            rotate(0, 0, 0)
            rotate(0, 0, 1)
            for m in range(FIRST):
                head(0, m, 0)
            with pool.Fori(0, LOOPS) as p:
                for s in range(FIRST, FIRST + PER_PAIR):
                    head(p * PER_PAIR, s, p)
            for s in range(FIRST + LOOPS * PER_PAIR, HEADS):
                head(0, s, 0, last_heads=True)

            h_low(1)

            def low_e(j, n):
                pool.wait_ge(whi_e, n)
                low(gu_lo[:, j], raw_gu[:, j], gu_hi[:, j])
                low(d_lo[:, j], raw_d[:, j], d_hi[:, j]).then_inc(wlo_e, 1)

            def step(base, s, grp, end=False):
                t = base + s
                pool.wait_ge(hv_hi_done, t + 1)
                low(hv_lo[:, s % 2], hv[:, s % 2], hv_hi[:, s % 2]).then_inc(hv_lo_done, 1)
                q = s // B + 2
                if s % B == 1 and not (end and q >= CH):
                    low_e(q % GROUP, grp * GROUP + (q + 1))

            low_e(0, 1)
            low_e(1, 2)
            for t in range(FIRST_STEP):
                step(0, t, 0)
            with pool.Fori(0, GROUPS - 1) as g:
                for s in range(FIRST_STEP, FIRST_STEP + PER_GROUP):
                    step(g * PER_GROUP, s, g)
            for t in range(FIRST_STEP + (GROUPS - 1) * PER_GROUP, STEPS):
                step(0, t, 0, end=True)


def kernel(L0_attn_x, L0_attn_wq, L0_attn_wk, L0_attn_wv, L0_attn_wo, L0_ffn_router_w,
           L0_ffn_w_gate, L0_ffn_w_up, L0_ffn_w_down, L0_c, L0_wmod):
    import concourse.bacc as bacc
    from concourse.bass_utils import run_bass_kernel_spmd

    a = [np.asarray(v) for v in (L0_attn_x, L0_attn_wq, L0_attn_wk, L0_attn_wv, L0_attn_wo, L0_ffn_router_w,
                                 L0_ffn_w_gate, L0_ffn_w_up, L0_ffn_w_down, L0_c, L0_wmod)]
    x, wq, wk, wv, wo, rw, wg, wu, wd, c, wmod = a
    flat = x.reshape(N, M)

    def halves(w):
        return w.reshape(C, P, -1).transpose(1, 0, 2)

    half = D // 2
    freqs = np.power(np.float32(10000.0), -(np.arange(half, dtype=np.float32) / np.float32(half)))
    rad = np.arange(T, dtype=np.float32)[:, None] * freqs[None, :]
    cos, sin = np.cos(rad).T, np.sin(rad).T
    cos2, sin2 = np.concatenate([cos, cos]), np.concatenate([sin, -sin])
    scale = np.float32(1.0 / D)
    bf = mybir.dt.np(BF16)
    q_i, k_i = np.arange(P)[:, None], np.arange(P)[None, :]
    qk = np.stack([wq, wk], 0).reshape(2, C, P, PAIRS, 2, D)
    gu = np.stack([wg, wu], 0).transpose(0, 2, 1, 3).reshape(2, C, P, CH, P)
    arrays = {
        "x": flat.reshape(NT, P, M).transpose(1, 0, 2),
        "xT": flat.T.reshape(C, P, N).transpose(1, 0, 2),
        "cT": halves(c.T),
        "wmod": halves(wmod),
        "rwT": halves(rw.T),
        "rope": np.stack([cos2 * scale, cos2, sin2 * scale, sin2], 1),
        "ident": np.eye(P, dtype=np.float32),
        "identb": np.eye(P).astype(bf),
        "maskb": np.where(q_i < k_i, -1e30, 0.0).astype(bf),
        "selb": np.tile(np.repeat(np.eye(E), I, axis=1), (3, 1)).astype(bf),
        "wqk": qk.transpose(3, 4, 2, 1, 0, 5),
        "wv": wv.reshape(C, P, PAIRS, 2 * D).transpose(2, 1, 0, 3),
        "wo": wo.reshape(PAIRS, 2, D, M).transpose(0, 2, 1, 3),
        "wgu": gu.transpose(3, 2, 1, 0, 4),
        "wd": wd.reshape(CH, P, M),
    }
    nc = bacc.Bacc("TRN2", target_bir_lowering=False, num_devices=1)
    arrays = {k: np.ascontiguousarray(v) for k, v in arrays.items()}
    aps = [nc.dram_tensor(k, v.shape, mybir.dt.from_np(v.dtype), kind="ExternalInput").ap() for k, v in arrays.items()]
    outT = nc.dram_tensor("outT", (P, C, N), F32, kind="ExternalOutput").ap()
    build(nc, *aps, outT)
    r = run_bass_kernel_spmd(nc, [arrays], core_ids=[0])
    y = r.results[0]["outT"]
    return np.ascontiguousarray(y.transpose(2, 1, 0)).reshape(B, T, M)
```

```python
import numpy as np
import concourse.bass as bass
from concourse import mybir
from contextlib import ExitStack

F32 = mybir.dt.float32
F32R = mybir.dt.float32r
BF16 = mybir.dt.bfloat16
ALU = mybir.AluOpType
ACT = mybir.ActivationFunctionType
AX = mybir.AxisListType

P = 128
B, T, M = 4, 512, 256
H, D = 16, 128
E, I, TOPK = 32, 96, 8
N = B * T
NT = N // P
TB = T // P
C = M // P
HEADS = B * H
PAIRS = H // 2
PER_PAIR = 2 * B
LOOPS = PAIRS - 1
FIRST = 3
CH = E * I // P
STEPS = CH * B
GROUP = 3
PER_GROUP = GROUP * B
GROUPS = CH // GROUP
EXPERTS = GROUP * P // I
E_OF = [(j * P // I, (j + 1) * P // I - (1 if (j + 1) * P % I == 0 else 0)) for j in range(GROUP)]
E_ROWS = [(e + 1) * I - j * P for j, (e, _) in enumerate(E_OF)]
FIRST_STEP = PER_GROUP + 3
EPS = 1e-5
KS = 3 * E
QB = [3, 2, 1, 0]
SA, CA, GA, SB_, CB, GB = range(6)
AFTER_GATE = {9: 6, 10: 8, 11: 10}
AFTER_UP = {3: 0, 4: 1, 5: 2, 6: 3, 7: 4, 8: 5, 9: 7, 10: 9, 11: 11}
Y_CREDIT = 4
ADD_CREDIT = 1


def build(nc, x, xT, cT, wmod, rwT, rope, ident, identb, maskf, selb, wqk, wv, wo, wgu, wd, w_dram, outT):
    ctx = ExitStack()
    with ctx:
        def sb(name, shape, dt=F32):
            return ctx.enter_context(nc.sbuf_tensor(name, shape, dt))

        def sem(name):
            return ctx.enter_context(nc.semaphore(name))

        accT = sb("accT", [P, C, N])
        hT_hi = sb("hT_hi", [P, C, N], F32R)
        hT_lo = sb("hT_lo", [P, C, N], F32R)
        xn = sb("xn", [P, NT, M])
        id_f = sb("id_f", [P, P])
        id_b = sb("id_b", [P, P], BF16)
        mask = sb("mask", [P, T])
        sel_b = sb("sel_b", [KS, E * I], BF16)
        rw_sb = sb("rw_sb", [P, C, E])
        c_sb = sb("c_sb", [P, C, B])
        c_silu = sb("c_silu", [P, C, B])
        mod = sb("mod", [P, 6 * C, B])
        gate = sb("gate", [P, 2, C, B])
        gsign = sb("gsign", [P, 2, C, B])
        gabs = sb("gabs", [P, 2, C, B])
        stats = sb("stats", [P, NT, 6])
        meanvar = sb("meanvar", [P, NT, 2])
        std = sb("std", [P, NT])
        rstd = sb("rstd", [P, NT])
        h_f = sb("h_f", [P, 4, T])
        wT_b = sb("wT_b", [KS, N], BF16)
        raw_gu = sb("raw_gu", [P, GROUP, C, 2, P])
        raw_d = sb("raw_d", [P, GROUP, M])

        att = ExitStack()

        def ab(name, shape, dt=F32):
            return att.enter_context(nc.sbuf_tensor(name, shape, dt))

        raw_qk = ab("raw_qk", [P, 2, C, 2, P])
        raw_v = ab("raw_v", [P, C, 2 * D])
        raw_o = ab("raw_o", [P, 2, M])
        qk_hi = ab("qk_hi", [P, 2, C, 2, P], F32R)
        qk_lo = ab("qk_lo", [P, 2, C, 2, P], F32R)
        v_hi = ab("v_hi", [P, C, 2 * D], F32R)
        v_lo = ab("v_lo", [P, C, 2 * D], F32R)
        rope_sb = ab("rope_sb", [P, 4, T])
        cosx = ab("cosx", [P, 2, T])
        sinx = ab("sinx", [P, 2, T])
        rot_f = ab("rot_f", [P, 2, T])
        rot_hi = ab("rot_hi", [P, 2, 2, T], F32R)
        rot_lo = ab("rot_lo", [P, 2, 2, T], F32R)
        o_hi = ab("o_hi", [P, 2, M], F32R)
        o_lo = ab("o_lo", [P, 2, M], F32R)
        prob = ab("prob", [P, TB, T])
        probT = ab("probT", [P, 2, TB, T])
        wmod_sb = probT[:, :, :, :].rearrange("p a k q -> p (a k q)")[:, 0:C * 6 * M].rearrange("p (c n) -> p c n", c=C)
        vals = ab("vals", [P, 2, TB, 2 * D])
        ao_hi = ab("ao_hi", [P, 2, 2, T], F32R)
        ao_lo = ab("ao_lo", [P, 2, 2, T], F32R)
        negmax = ab("negmax", [P, 2, TB])
        rowsum = ab("rowsum", [P, 2, TB])
        rinv = ab("rinv", [P, 2, TB])
        att.close()

        gu_hi = sb("gu_hi", [P, GROUP, C, 2, P], F32R)
        gu_lo = sb("gu_lo", [P, GROUP, C, 2, P], F32R)
        d_hi = sb("d_hi", [P, GROUP, M], F32R)
        d_lo = sb("d_lo", [P, GROUP, M], F32R)
        h2_f = sb("h2_f", [P, C, N])
        w_rows = sb("w_rows", [E, N])
        logit = sb("logit", [P, NT, E])
        lmax = sb("lmax", [P, NT])
        ex = sb("ex", [P, NT, E])
        top = sb("top", [P, NT, TOPK])
        rest = sb("rest", [P, NT, E])
        wsum = sb("wsum", [P, NT])
        winv = sb("winv", [P, NT])
        w_f = sb("w_f", [P, NT, E])
        w_r = sb("w_r", [P, NT, E])
        w_b = sb("w_b", [P, NT, 3, E], BF16)
        w_ring = sb("w_ring", [P, GROUP, N])
        sil = sb("sil", [P, 2, T])
        silw = sb("silw", [P, 2, T])
        hv = sb("hv", [P, 2, T])
        hv_hi = sb("hv_hi", [P, 2, T], F32R)
        hv_lo = sb("hv_lo", [P, 2, T], F32R)

        PS = ctx.enter_context(nc.psum_tensor("PS", [P, 8, T], F32))
        QKp = PS[:, 0:2, :]
        Sp = PS[:, 2:4, :]
        Tp = PS[:, 4:6, :]
        Op = PS[:, 6, :]
        VYp = PS[:, 7, :]

        ld_x = [sem(f"ld_x{b}") for b in range(B)]
        ld_c = sem("ld_c")
        ld_mod = sem("ld_mod")
        ld_mod2 = sem("ld_mod2")
        ld_id = sem("ld_id")
        ld_rope = sem("ld_rope")
        ld_mask = sem("ld_mask")
        ld_router = sem("ld_router")
        ld_sel = sem("ld_sel")
        ld_acc = sem("ld_acc")
        ld_qk = sem("ld_qk")
        ld_v = sem("ld_v")
        ld_o = sem("ld_o")
        ld_e = [sem(f"ld_e{j}") for j in range(GROUP)]
        ld_w = [sem(f"ld_w{j}") for j in range(GROUP)]
        expanded = sem("expanded")
        w_copied = sem("w_copied")
        w_stored = sem("w_stored")
        stored = sem("stored")
        dve_step = sem("dve_step")
        silu_c = sem("silu_c")
        mod_done = sem("mod_done")
        mod_ready = sem("mod_ready")
        var_ready = sem("var_ready")
        std_ready = sem("std_ready")
        normed_x = sem("normed_x")
        ln_turned = sem("ln_turned")
        h_ready = sem("h_ready")
        h_hi = sem("h_hi")
        h_lo = sem("h_lo")
        whi_qk = sem("whi_qk")
        wlo_qk = sem("wlo_qk")
        whi_v = sem("whi_v")
        wlo_v = sem("wlo_v")
        whi_o = sem("whi_o")
        wlo_o = sem("wlo_o")
        qk_done = sem("qk_done")
        roped = sem("roped")
        rotated = sem("rotated")
        rot_hi_done = sem("rot_hi_done")
        rot_lo_done = sem("rot_lo_done")
        scored = sem("scored")
        maxed = sem("maxed")
        exped = sem("exped")
        inverted = sem("inverted")
        scaled = sem("scaled")
        turned = sem("turned")
        pt_out = sem("pt_out")
        v_done = sem("v_done")
        v_out = sem("v_out")
        pv_done = sem("pv_done")
        ao_hi_done = sem("ao_hi_done")
        ao_lo_done = sem("ao_lo_done")
        projected = sem("projected")
        added = sem("added")
        x1_turned = sem("x1_turned")
        x1_measured = sem("x1_measured")
        x1_copied = sem("x1_copied")
        h2_ready = sem("h2_ready")
        logits_done = sem("logits_done")
        shifted = sem("shifted")
        ex_done = sem("ex_done")
        w_split = sem("w_split")
        wT_done = sem("wT_done")
        wT_ready = sem("wT_ready")
        whi_e = sem("whi_e")
        wlo_e = sem("wlo_e")
        g_done = sem("g_done")
        wb_done = sem("wb_done")
        u_done = sem("u_done")
        down_done = sem("down_done")
        sil_done = sem("sil_done")
        silw_done = sem("silw_done")
        hv_done = sem("hv_done")
        hv_hi_done = sem("hv_hi_done")
        hv_lo_done = sem("hv_lo_done")
        y_added = sem("y_added")

        block = ctx.enter_context(nc.Block())

        def reach(eng, s, v):
            if not isinstance(v, int) or v > 0:
                eng.wait_ge(s, v)

        def place(s):
            return (s % GROUP, s // GROUP) if s < PER_GROUP else ((s // B) % GROUP, s % B)

        def x1_bank(u):
            return (0, 0, 1, 0, 2, 3, 6, 7)[u]

        def h2_bank(i):
            return (0, 1, 4, 5, 5, 5, 5, 5)[i]

        def cols(b):
            return slice(b * T, (b + 1) * T)

        @block.sync
        def _(sp):
            def load_x(b):
                sp.dma_start(xn[:, b * TB:(b + 1) * TB, :], x[:, b * TB:(b + 1) * TB, :]).then_inc(ld_x[b], 16)

            load_x(0)
            sp.dma_start(c_sb[:, :, :], cT).then_inc(ld_c, 16)
            sp.dma_start(wmod_sb[:, :, 0:2 * M], wmod[:, :, 0:2 * M]).then_inc(ld_mod, 16)
            sp.dma_start(id_f[:, :], ident).then_inc(ld_id, 16)
            sp.dma_start(raw_qk[:, 0], wqk[0, 0]).then_inc(ld_qk, 16)
            load_x(1)
            sp.dma_start(raw_qk[:, 1], wqk[0, 1]).then_inc(ld_qk, 16)
            load_x(2)
            sp.dma_start(rope_sb[:, :, :], rope).then_inc(ld_rope, 16)
            sp.dma_start(raw_v[:, :, :], wv[0]).then_inc(ld_v, 16)
            sp.dma_start(wmod_sb[:, :, 2 * M:6 * M], wmod[:, :, 2 * M:6 * M]).then_inc(ld_mod2, 16)
            load_x(3)
            sp.dma_start(id_b[:, :], identb).then_inc(ld_mask, 16)
            sp.dma_start(mask[:, :], maskf).then_inc(ld_mask, 16)
            sp.dma_start(raw_o[:, :, :], wo[0]).then_inc(ld_o, 16)
            sp.dma_start(accT[:, :, :], xT).then_inc(ld_acc, 16)
            sp.dma_start(rw_sb[:, :, :], rwT).then_inc(ld_router, 16)
            sp.dma_start(sel_b[:, :], selb).then_inc(ld_sel, 16)
            for q in range(GROUP):
                sp.dma_start(raw_gu[:, q], wgu[q]).then_inc(ld_e[q], 16)
                sp.dma_start(raw_d[:, q], wd[q]).then_inc(ld_e[q], 16)
            with sp.Fori(0, LOOPS) as p:
                for j in range(2):
                    sp.wait_ge(wlo_qk, p * 2 + (j + 1))
                    sp.dma_start(raw_qk[:, j], wqk[p + 1, j]).then_inc(ld_qk, 16)
                sp.wait_ge(wlo_v, p + 1)
                sp.dma_start(raw_v[:, :, :], wv[p + 1]).then_inc(ld_v, 16)
                sp.wait_ge(wlo_o, p + 1)
                sp.dma_start(raw_o[:, :, :], wo[p + 1]).then_inc(ld_o, 16)
            def load_expert(g, j, x):
                sp.wait_ge(wlo_e, g * GROUP + (j + 1))
                sp.dma_start(raw_gu[:, j], wgu[x + GROUP]).then_inc(ld_e[j], 16)
                sp.dma_start(raw_d[:, j], wd[x + GROUP]).then_inc(ld_e[j], 16)

            def load_weights(g, j, tok):
                first, second = E_OF[j]
                n = E_ROWS[j]
                for e, rows in ((first, slice(0, n)), (second, slice(n, P))):
                    src = w_dram[e:e + 1, tok] if isinstance(g, int) and g == 0 else \
                        w_dram[bass.ds(g * EXPERTS + e, 1), tok]
                    sp.dma_start(w_ring[rows, j, tok],
                                 src.broadcast_to([rows.stop - rows.start, tok.stop - tok.start])).then_inc(ld_w[j], 16)

            for j in range(GROUP):
                load_expert(0, j, j)
            for half in range(2):
                sp.wait_ge(w_copied, 2 * half + 2)
                tok = slice(half * N // 2, (half + 1) * N // 2)
                sp.dma_start(w_dram[:, tok], w_rows[:, tok]).then_inc(w_stored, 16)
            sp.wait_ge(w_stored, 32)
            load_weights(1, 0, cols(B - 1))
            for j in range(1, GROUP):
                load_weights(1, j, slice(0, N))
            for j in range(GROUP):
                load_expert(1, j, GROUP + j)
            with sp.Fori(2, GROUPS - 1) as g:
                for j in range(GROUP):
                    load_expert(g, j, g * GROUP + j)
                    sp.wait_ge(silw_done, g * PER_GROUP + (j - 2) * B)
                    load_weights(g, j, slice(0, N))
            for j in range(GROUP):
                sp.wait_ge(silw_done, (GROUPS - 1) * PER_GROUP + (j - 2) * B)
                load_weights(GROUPS - 1, j, slice(0, N))
            for b in range(B - 1):
                sp.wait_ge(y_added, STEPS - B + b + 1)
                sp.dma_start(outT[:, :, cols(b)], accT[:, :, cols(b)]).then_inc(stored, 16)
            for c in range(C):
                sp.wait_ge(y_added, STEPS - 1 + c + 1)
                sp.dma_start(outT[:, c, cols(B - 1)], accT[:, c, cols(B - 1)]).then_inc(stored, 16)
            sp.wait_ge(stored, 16 * (B - 1 + C))

        @block.tensor
        def _(pe):
            def mm3(out, hi, lo, rhs_hi, rhs_lo, k, n):
                nc.tensor.matmul(out, hi, rhs_hi, start=(k == 0), stop=False)
                nc.tensor.matmul(out, hi, rhs_lo, start=False, stop=False)
                return nc.tensor.matmul(out, lo, rhs_hi, start=False, stop=(k == n - 1))

            def modulation(q0, q1):
                for q in range(q0, q1):
                    for c in range(C):
                        last = nc.tensor.matmul(Op[:, q * B:(q + 1) * B], wmod_sb[:, c, q * P:(q + 1) * P],
                                                c_silu[:, c, :], start=(c == 0), stop=(c == C - 1))
                last.then_inc(mod_done, 1)

            def turn_h(i, bank):
                b, c = divmod(i % (B * C), C)
                pe.wait_ge(normed_x, NT * (i // (B * C)) + (b + 1) * TB)
                for t in range(TB):
                    last = nc.tensor.transpose(PS[:, bank, t * P:(t + 1) * P],
                                               xn[:, b * TB + t, c * P:(c + 1) * P], id_f[:, :])
                last.then_inc(ln_turned, 1)

            def turn_x1(u):
                for i in range(2 * u, 2 * u + 2):
                    for c in range(C):
                        o = (i % 2) * M + c * P
                        last = nc.tensor.transpose(PS[:, x1_bank(u), o:o + P], accT[:, c, i * P:(i + 1) * P], id_f[:, :])
                last.then_inc(x1_turned, 1)

            pe.wait_ge(ld_mod, 16)
            pe.wait_ge(silu_c, 1)
            modulation(0, 2 * C)
            pe.wait_ge(ld_id, 16)
            for t in range(TB):
                pe.wait_ge(normed_x, t + 1)
                for c in range(C):
                    last = nc.tensor.transpose(PS[:, 4 + c, t * P:(t + 1) * P], xn[:, t, c * P:(c + 1) * P], id_f[:, :])
                    if t == TB - 1:
                        last.then_inc(ln_turned, 1)

            def proj_qk(j, b, k, first=False):
                for c in range(C):
                    if first:
                        pe.wait_ge(h_lo, c + 1)
                    last = mm3(QKp[:, k], qk_hi[:, j, c, k], qk_lo[:, j, c, k],
                               hT_hi[:, c, cols(b)], hT_lo[:, c, cols(b)], c, C)
                last.then_inc(qk_done, 1)

            def proj_v(b, half):
                for t in range(2):
                    tok = slice(b * T + (2 * half + t) * P, b * T + (2 * half + t + 1) * P)
                    for c in range(C):
                        last = mm3(VYp[:, t * 2 * D:(t + 1) * 2 * D], hT_hi[:, c, tok], hT_lo[:, c, tok],
                                   v_hi[:, c, :], v_lo[:, c, :], c, C)
                last.then_inc(v_done, 1)

            def attend_v(par, j, upar):
                for kt in range(TB):
                    last = nc.tensor.matmul(Op[:, kt * P:T], vals[:, upar, kt, j * D:(j + 1) * D],
                                            probT[:, par, kt, kt * P:T], start=(kt == 0), stop=(kt == TB - 1))
                last.then_inc(pv_done, 1)

            def proj_o(upar, c):
                for j in range(2):
                    last = mm3(VYp, o_hi[:, j, c * P:(c + 1) * P], o_lo[:, j, c * P:(c + 1) * P],
                               ao_hi[:, upar, j, :], ao_lo[:, upar, j, :], j, 2)
                last.then_inc(projected, 1)

            def head(base, s, last_heads=False):
                m = base + s
                par = s % 2
                steady = not isinstance(m, int)

                def score(o):
                    qb = QB[o]
                    w = max(qb + 1, 2) * P
                    if o == 0:
                        pe.wait_ge(rot_lo_done, m * 2 + 2)
                    reach(pe, exped, m * 4 + (o - 1) if not isinstance(m, int) or m * 4 + o - 1 > 0 else 0)
                    q = slice(qb * P, (qb + 1) * P)
                    mm3(Sp[:, o % 2, 0:w], rot_hi[:, par, 0, q], rot_lo[:, par, 0, q],
                        rot_hi[:, par, 1, 0:w], rot_lo[:, par, 1, 0:w], 0, 1).then_inc(scored, 1)

                def turn(o):
                    qb = QB[o]
                    pe.wait_ge(scaled, m * 4 + (o + 1))
                    reach(pe, pt_out, m * 4 + (o - 1) if not isinstance(m, int) or m > 0 else o - 1)
                    for kt in range(qb + 1):
                        last = nc.tensor.transpose(Tp[:, o % 2, kt * P:(kt + 1) * P],
                                                   prob[:, qb, kt * P:(kt + 1) * P], id_f[:, :])
                    last.then_inc(turned, 1)

                def qk(hs, k):
                    if last_heads and hs >= HEADS:
                        return
                    nj, nb = hs % 2, hs % PER_PAIR // 2
                    if k == 0 and nb == 0:
                        pe.wait_ge(wlo_qk, pair * 2 + (hs // PER_PAIR * 2 + nj + 1))
                    if k == 0 and nj == 0 and isinstance(m, int) and hs < PER_PAIR:
                        pe.wait_ge(h_lo, (nb + 1) * C)
                    pe.wait_ge(roped, m * 2 + (2 * (hs - s) + k - 1))
                    proj_qk(nj, nb, k)

                pair = base_pair[0]
                if last_heads and s == HEADS - 1:
                    pe.wait_ge(added, HEADS - 4 + ADD_CREDIT)
                    pe.wait_ge(roped, 2 * HEADS)
                    turn_x1(2)
                score(0)
                score(1)
                if last_heads and s == HEADS - 2:
                    pe.wait_ge(roped, 2 * HEADS - 1)
                    turn_x1(0)
                if last_heads and s == HEADS - 1:
                    pe.wait_ge(x1_copied, 2)
                    turn_x1(3)
                if s in (1, 2) and isinstance(m, int):
                    i = (s + 1) * C
                    pe.wait_ge(v_out, s + 2)
                    turn_h(i, 7)
                qk(s + 1, 1)
                if isinstance(m, int) and m == 0:
                    pe.wait_ge(v_out, 1)
                    proj_v(0, 1)
                if not steady:
                    score(2)
                if s in (1, 2) and isinstance(m, int):
                    pe.wait_ge(h_ready, i + 1)
                    turn_h(i + 1, 7)
                if not isinstance(m, int) or m >= 1:
                    pe.wait_ge(pt_out, m * 4)
                    pe.wait_ge(v_out, m + 1)
                    reach(pe, ao_lo_done, m - 1 if not isinstance(m, int) or m > 1 else 0)
                    if isinstance(m, int) and m == 1:
                        pe.wait_ge(mod_ready, 2)
                    attend_v(1 - par, (s - 1) % 2, ((s - 1) // 2) % 2)
                if steady:
                    score(2)
                turn(0)
                score(3)
                if not last_heads or s < HEADS - 2:
                    v = (s + 2) % PER_PAIR
                    if v == 0:
                        pe.wait_ge(wlo_v, pair + ((s + 2) // PER_PAIR + 1))
                    if not isinstance(m, int) or m >= 3:
                        pe.wait_ge(added, m + (ADD_CREDIT - 2))
                    if isinstance(m, int) and m <= 2:
                        pe.wait_ge(h_lo, 2 * C)
                        pe.wait_ge(h_ready, (m + 2) * C)
                    if isinstance(m, int) and m == 2:
                        pe.wait_ge(h_lo, 3 * C)
                    pe.wait_ge(v_out, m + 2)
                    proj_v(v // 2, v % 2)
                turn(1)
                turn(2)
                qk(s + 2, 0)
                if last_heads and s == HEADS - 2:
                    pe.wait_ge(x1_copied, 1)
                    turn_x1(1)
                if not isinstance(m, int) or m >= 2:
                    y_stage(m - 2, s - 2, pair, last_heads)
                turn(3)

            def y_stage(y, s, pair, last_heads=False):
                if s % PER_PAIR == 0:
                    pe.wait_ge(wlo_o, s // PER_PAIR + 1 if isinstance(y, int) else pair + (s // PER_PAIR + 1))
                pe.wait_ge(ao_lo_done, y + (2 - s % 2))
                pe.wait_ge(added, y + ADD_CREDIT)
                pe.wait_ge(v_out, min(y + 5, HEADS) if isinstance(y, int) else y + 5)
                proj_o((s // 2) % 2, s % 2)

            base_pair = [0]
            pe.sem_inc(projected, Y_CREDIT)
            pe.wait_ge(wlo_qk, 1)
            proj_qk(0, 0, 0, first=True)
            proj_qk(0, 0, 1)
            for i in range(C, 2 * C):
                pe.wait_ge(h_ready, i - 1)
                turn_h(i, 4 + i % 2)
            pe.wait_ge(wlo_v, 1)
            pe.wait_ge(wlo_qk, 2)
            pe.wait_ge(roped, 1)
            proj_qk(1, 0, 0)
            pe.wait_ge(wlo_v, 1)
            proj_v(0, 0)
            pe.wait_ge(ld_mod2, 16)
            modulation(2 * C, 6 * C)
            for m in range(FIRST):
                head(0, m)
            pe.wait_ge(h_lo, B * C)
            with pe.Fori(0, LOOPS) as p:
                base_pair[0] = p
                for s in range(FIRST, FIRST + PER_PAIR):
                    head(p * PER_PAIR, s)
            base_pair[0] = 0
            for s in range(FIRST + LOOPS * PER_PAIR, HEADS):
                head(0, s, last_heads=True)
            pe.wait_ge(pt_out, 4 * HEADS)
            pe.wait_ge(ao_lo_done, HEADS - 1)
            attend_v(1, 1, 1)
            pe.wait_ge(added, HEADS - 2 + ADD_CREDIT)
            turn_x1(4)
            turn_x1(5)
            turn_h(B * C, h2_bank(0))
            turn_h(B * C + 1, h2_bank(1))
            y_stage(HEADS - 2, HEADS - 2, 0)
            y_stage(HEADS - 1, HEADS - 1, 0)

            def logits(half):
                pe.wait_ge(h2_ready, 2 * C * (half + 1))
                pe.wait_ge(ld_router, 16)
                for i in range(NT // 2):
                    tok = slice((half * NT // 2 + i) * P, (half * NT // 2 + i + 1) * P)
                    for c in range(C):
                        last = nc.tensor.matmul(PS[:, 5, i * E:(i + 1) * E], h2_f[:, c, tok], rw_sb[:, c, :],
                                                start=(c == 0), stop=(c == C - 1))
                last.then_inc(logits_done, 1)

            def turn_w(half):
                pe.wait_ge(w_split, half + 1)
                pe.wait_ge(ld_mask, 32)
                wps = PS[:, 5, :].bitcast(BF16)
                for i in range(NT // 2):
                    last = nc.tensor.transpose(wps[0:KS, i * P:(i + 1) * P],
                                               w_b[:, half * NT // 2 + i].rearrange("p s e -> p (s e)"), id_b[:, :])
                last.then_inc(wT_done, 1)

            for i in range(2, 2 * C):
                turn_h(B * C + i, h2_bank(i))
            pe.wait_ge(added, HEADS + ADD_CREDIT)
            turn_x1(6)
            turn_x1(7)
            logits(0)

            def gate_up(j, b, k, t):
                bank = (0 if k == 0 else 2) + t % 2
                for c in range(C):
                    last = mm3(PS[:, bank], gu_hi[:, j, c, k], gu_lo[:, j, c, k],
                               hT_hi[:, c, cols(b)], hT_lo[:, c, cols(b)], c, C)
                return last

            def down(j, par):
                for c in range(C):
                    last = mm3(PS[:, 6 + c], d_hi[:, j, c * P:(c + 1) * P], d_lo[:, j, c * P:(c + 1) * P],
                               hv_hi[:, par], hv_lo[:, par], 0, 1)
                last.then_inc(down_done, 1)

            def select(base, s, grp):
                t = base + s
                j, b = place(s)
                chunk = j if s < PER_GROUP else s // B
                sel = sel_b[:, chunk * P:(chunk + 1) * P]
                bank = 4 + s % 2 if s >= PER_GROUP else 4
                if s < PER_GROUP:
                    pe.wait_ge(wT_ready, b // 2 + 1)
                if s == PER_GROUP + 1:
                    pe.wait_ge(w_copied, B)
                if s <= PER_GROUP:
                    reach(pe, hv_done, t)
                else:
                    pe.wait_ge(silw_done, t - 1)
                nc.tensor.matmul(PS[:, bank], sel, wT_b[:, cols(b)], start=True, stop=True).then_inc(wb_done, 1)

            def step(base, s, grp):
                t = base + s
                j, b = place(s)
                if b == 0:
                    pe.wait_ge(wlo_e, grp + (s // B + 1) if isinstance(base, int) else grp * GROUP + (s // B + 1))
                reach(pe, sil_done, t - 1)
                gate_up(j, b, 0, s).then_inc(g_done, 1)
                if s < FIRST_STEP:
                    select(base, s, grp)
                pe.wait_ge(hv_done, t - 1)
                gate_up(j, b, 1, s).then_inc(u_done, 1)
                down_stage(t - 1, s - 1)

            def down_stage(t, s):
                pe.wait_ge(hv_lo_done, t + 1)
                reach(pe, y_added, t)
                down(place(s)[0], s % 2)

            def expand(b):
                if b == 0:
                    pe.wait_ge(ld_sel, 16)
                reach(pe, w_copied, b)
                pe.wait_ge(wT_ready, b // 2 + 1)
                nc.tensor.matmul(PS[0:E, 5, :], sel_b[:, :].rearrange("k (e i) -> k e i", i=I)[:, :, 0],
                                 wT_b[:, cols(b)], start=True, stop=True).then_inc(expanded, 1)

            def weigh(u):
                if u == 0:
                    pe.wait_ge(ld_sel, 16)
                select(0, u, 0)
                if u == 1:
                    pe.wait_ge(x1_copied, NT // 2)
                if u > 0:
                    down_stage(u - 1, u - 1)

            def turn_h2_late(i):
                reach(pe, h2_ready, i if i > 2 * C else 0)
                turn_h(B * C + i, h2_bank(i))

            for t in range(PER_GROUP):
                j, b = place(t)
                if t < GROUP:
                    pe.wait_ge(wlo_e, t + 1)
                if j == 0:
                    pe.wait_ge(h_lo, B * C + C * (b + 1))
                reach(pe, sil_done, t - 1)
                gate_up(j, b, 0, t).then_inc(g_done, 1)
                if t == 3:
                    turn_w(0)
                if t == 6:
                    logits(1)
                if t in AFTER_GATE:
                    weigh(AFTER_GATE[t])
                if t == 7:
                    pe.wait_ge(shifted, 2)
                    expand(0)
                if t == 8:
                    expand(1)
                if t == 10:
                    expand(3)
                if t < 2:
                    pe.wait_ge(x1_copied, t + 5)
                reach(pe, silw_done, t - 1)
                gate_up(j, b, 1, t).then_inc(u_done, 1)
                if t == 4:
                    pe.wait_ge(wT_ready, 1)
                    turn_h2_late(4)
                if t == 5:
                    turn_h2_late(6)
                if t == 9:
                    expand(2)
                if t in AFTER_UP:
                    weigh(AFTER_UP[t])
                if t == 8:
                    pe.wait_ge(w_copied, 2)
                    turn_w(1)
                if t == 4:
                    turn_h2_late(5)
                if t == 5:
                    turn_h2_late(7)
            for t in range(PER_GROUP, FIRST_STEP):
                step(0, t, 0)
            with pe.Fori(0, GROUPS - 2) as g:
                for s in range(FIRST_STEP, FIRST_STEP + PER_GROUP):
                    step(g * PER_GROUP, s, g)
            for t in range(FIRST_STEP + (GROUPS - 2) * PER_GROUP, STEPS):
                step(0, t, 0)
            down_stage(STEPS - 1, STEPS - 1)

        @block.scalar
        def _(act):
            act.wait_ge(ld_c, 16)
            nc.scalar.activation(c_silu[:, :, :], c_sb[:, :, :], ACT.Silu).then_inc(silu_c, 1)

            def split_qk(j, n, used):
                act.wait_ge(ld_qk, n)
                reach(act, qk_done, used)
                nc.scalar.activation(qk_hi[:, j], raw_qk[:, j], ACT.Copy).then_inc(whi_qk, 1)

            def split_v(n, used):
                act.wait_ge(ld_v, n)
                reach(act, v_done, used)
                nc.scalar.activation(v_hi[:, :, :], raw_v[:, :, :], ACT.Copy).then_inc(whi_v, 1)

            def split_o(n, used):
                act.wait_ge(ld_o, n)
                reach(act, projected, used)
                nc.scalar.activation(o_hi[:, :, :], raw_o[:, :, :], ACT.Copy).then_inc(whi_o, 1)

            def h_high(b):
                for c in range(C):
                    i = b * C + c
                    act.wait_ge(h_ready, i + 1)
                    nc.scalar.activation(hT_hi[:, c, cols(b)], h_f[:, i % 4], ACT.Copy).then_inc(h_hi, 1)

            def deviation(n, t0, t1):
                act.wait_ge(var_ready, n)
                nc.scalar.activation(std[:, t0:t1], std[:, t0:t1], ACT.Sqrt).then_inc(std_ready, 1)

            deviation(1, 0, TB)
            act.wait_ge(ld_qk, 32)
            nc.scalar.activation(qk_hi[:, 0], raw_qk[:, 0], ACT.Copy).then_inc(whi_qk, 1)
            h_high(0)
            nc.scalar.activation(qk_hi[:, 1], raw_qk[:, 1], ACT.Copy).then_inc(whi_qk, 1)
            split_v(16, 0)
            deviation(2, TB, 2 * TB)

            def split_e(j, n, used):
                act.wait_ge(ld_e[j], n)
                reach(act, down_done, used)
                nc.scalar.activation(gu_hi[:, j], raw_gu[:, j], ACT.Copy)
                nc.scalar.activation(d_hi[:, j], raw_d[:, j], ACT.Copy).then_inc(whi_e, 1)

            def v_copy(v, s):
                act.wait_ge(v_done, v + 1)
                if not isinstance(v, int) or v >= 4:
                    act.wait_ge(pv_done, v - (2 + s % 2))
                nc.scalar.activation(vals[:, (s // 2) % 2, 2 * (s % 2):2 * (s % 2) + 2, :],
                                     VYp.rearrange("p (t d) -> p t d", t=2), ACT.Copy).then_inc(v_out, 1)

            def head(base, s, pair, last_heads=False):
                m = base + s
                par = s % 2
                steady = not isinstance(m, int)

                def exp(o):
                    qb = QB[o]
                    w = (qb + 1) * P
                    act.wait_ge(maxed, m * 4 + (o + 1))
                    reach(act, turned, m * 4 + (o - 3) if not isinstance(m, int) or m > 0 else 0)
                    nc.scalar.activation(prob[:, qb, 0:w], Sp[:, o % 2, 0:w], ACT.Exp, bias=negmax[:, par, o:o + 1],
                                         scale=-1.0, accum_out=rowsum[:, par, o:o + 1]).then_inc(exped, 1)

                def pt_copy(o):
                    qb = QB[o]
                    act.wait_ge(turned, m * 4 + (o + 1))
                    reach(act, pv_done, m - 1 if not isinstance(m, int) or m > 1 else 0)
                    nc.scalar.activation(probT[:, par, 0:qb + 1, qb * P:(qb + 1) * P],
                                         Tp[:, o % 2, 0:(qb + 1) * P].rearrange("p (k q) -> p k q", q=P),
                                         ACT.Copy).then_inc(pt_out, 1)

                if s % PER_PAIR == 2:
                    nl = s // PER_PAIR
                    split_o(pair * 16 + 16 * (nl + 1), pair * 8 + (8 * nl + Y_CREDIT))
                more = not last_heads or s < HEADS - 1
                exp(0)
                exp(1)
                if last_heads and s == HEADS - 1:
                    copy_x1(2)
                if isinstance(m, int) and m == 0:
                    v_copy(1, 1)
                if more:
                    rot_high(m + 1, s + 1, 0)
                if steady:
                    out_high(m - 1, s - 1)
                exp(2)
                if last_heads and s == HEADS - 2:
                    copy_x1(0)
                if last_heads and s == HEADS - 1:
                    copy_x1(3)
                if isinstance(m, int) and m in (1, 2):
                    h_high(m + 1)
                if not steady and m >= 1:
                    out_high(m - 1, s - 1)
                pt_copy(0)
                if steady:
                    v_copy(m + 2, s + 2)
                exp(3)
                if more:
                    rot_high(m + 1, s + 1, 1)
                if not steady and s < HEADS - 2:
                    v_copy(m + 2, s + 2)
                if last_heads and s == HEADS - 1:
                    deviation(4, 0, NT // 2)
                pt_copy(1)
                pt_copy(2)
                pt_copy(3)
                if not last_heads:
                    nl = s // PER_PAIR
                    r = s % PER_PAIR
                    if r == 5:
                        split_v(pair * 16 + 16 * (nl + 2), pair * 8 + 8 * (nl + 1))
                        split_qk(0, pair * 32 + 32 * (nl + 2), pair * 16 + (16 * nl + 14))
                    if r == 6:
                        split_qk(1, pair * 32 + 32 * (nl + 2), pair * 16 + (16 * nl + 16))
                if last_heads and s == HEADS - 2:
                    act.wait_ge(qk_done, 2 * HEADS)
                    act.wait_ge(v_done, HEADS)
                    act.wait_ge(wlo_o, PAIRS)
                    copy_x1(1)
                    split_e(0, 32, 0)
                    split_e(1, 32, 0)
                if last_heads and s == HEADS - 1:
                    split_e(2, 32, 0)

            def copy_x1(u):
                act.wait_ge(x1_measured, u + 1)
                nc.scalar.activation(xn[:, 2 * u:2 * u + 2, :],
                                     PS[:, x1_bank(u)].rearrange("p (t m) -> p t m", t=2),
                                     ACT.Copy).then_inc(x1_copied, 1)

            def rot_high(h, s, k):
                act.wait_ge(rotated, h * 2 + (k + 1))
                reach(act, scored, h * 4 - 4 if not isinstance(h, int) or h > 1 else 0)
                nc.scalar.activation(rot_hi[:, s % 2, k], rot_f[:, k], ACT.Copy).then_inc(rot_hi_done, 1)

            def out_high(h, s):
                act.wait_ge(pv_done, h + 1)
                act.wait_ge(projected, h + (Y_CREDIT - 2 - s % 2))
                nc.scalar.activation(ao_hi[:, (s // 2) % 2, s % 2, :], Op, ACT.Copy).then_inc(ao_hi_done, 1)

            rot_high(0, 0, 0)
            rot_high(0, 0, 1)
            h_high(1)
            v_copy(0, 0)
            deviation(3, 2 * TB, NT)
            for m in range(FIRST):
                head(0, m, 0)
            with act.Fori(0, LOOPS) as p:
                for s in range(FIRST, FIRST + PER_PAIR):
                    head(p * PER_PAIR, s, p)
            for s in range(FIRST + LOOPS * PER_PAIR, HEADS):
                head(0, s, 0, last_heads=True)
            out_high(HEADS - 1, HEADS - 1)

            def modulate(i):
                b, c = divmod(i, C)
                act.wait_ge(ln_turned, B * C + i + 1)
                nc.scalar.activation(h2_f[:, c, cols(b)], PS[:, h2_bank(i)], ACT.Identity,
                                     bias=mod[:, SB_ * C + c, b:b + 1],
                                     scale=mod[:, CB * C + c, b:b + 1]).then_inc(h2_ready, 1)

            def high2(i):
                b, c = divmod(i, C)
                act.wait_ge(h2_ready, i + 1)
                nc.scalar.activation(hT_hi[:, c, cols(b)], h2_f[:, c, cols(b)], ACT.Copy).then_inc(h_hi, 1)

            def router_exp(half):
                act.wait_ge(shifted, half + 1)
                t = slice(half * NT // 2, (half + 1) * NT // 2)
                nc.scalar.activation(ex[:, t, :], logit[:, t, :], ACT.Exp).then_inc(ex_done, 1)

            def silu(t, s):
                act.wait_ge(g_done, t + 1)
                reach(act, silw_done, t - 1)
                nc.scalar.activation(sil[:, s % 2], PS[:, s % 2], ACT.Silu).then_inc(sil_done, 1)

            def copy_w(b):
                act.wait_ge(expanded, b + 1)
                nc.scalar.activation(w_rows[:, cols(b)], PS[0:E, 5, :], ACT.Copy).then_inc(w_copied, 1)

            def high(t, s):
                act.wait_ge(hv_done, t + 1)
                reach(act, down_done, t - 1)
                nc.scalar.activation(hv_hi[:, s % 2], hv[:, s % 2], ACT.Copy).then_inc(hv_hi_done, 1)

            def step(base, s, grp, end=False):
                t = base + s
                silu(t, s)
                high(t, s)
                q = s // B + 2
                if s >= PER_GROUP and s % B == 1 and not (end and q >= CH):
                    split_e(q % GROUP, grp * 32 + 32 * (q // GROUP + 1), base + (s - 1))

            for i in range(C):
                modulate(i)
            for i in range(C):
                high2(i)
            copy_x1(4)
            copy_x1(5)
            for i in range(C, 2 * C):
                modulate(i)
            for i in range(C, 2 * C):
                high2(i)
            router_exp(0)
            copy_x1(6)
            copy_x1(7)
            deviation(5, NT // 2, NT)
            for t in range(PER_GROUP):
                if t in (5, 6):
                    high2(2 * t - 6)
                    high2(2 * t - 5)
                if t == 7:
                    router_exp(1)
                silu(t, t)
                if t in (4, 5):
                    modulate(2 * t - 4)
                if t == 8:
                    copy_w(1)
                if t in AFTER_GATE:
                    high(AFTER_GATE[t], AFTER_GATE[t])
                if t == 10:
                    copy_w(3)
                if t == 11:
                    split_e(0, 64, 10)
                if t == 7:
                    copy_w(0)
                if t == 9:
                    copy_w(2)
                if t in AFTER_UP:
                    high(AFTER_UP[t], AFTER_UP[t])
                if t in (4, 5):
                    modulate(2 * t - 3)
            split_e(1, 64, 11)
            for t in range(PER_GROUP, FIRST_STEP):
                step(0, t, 0)
            with act.Fori(0, GROUPS - 2) as g:
                for s in range(FIRST_STEP, FIRST_STEP + PER_GROUP):
                    step(g * PER_GROUP, s, g)
            for t in range(FIRST_STEP + (GROUPS - 2) * PER_GROUP, STEPS):
                step(0, t, 0, end=True)

        @block.vector
        def _(dve):
            chain = [0]

            def settle(ins):
                chain[0] += 1
                ins.then_inc(dve_step, 1)
                dve.wait_ge(dve_step, chain[0])

            def measure(t, src):
                return nc.vector.bn_stats(stats[:, t, :], src)

            def variances(t0, t1):
                for t in range(t0, t1):
                    last = nc.vector.bn_aggr(meanvar[:, t, :], stats[:, t, :])
                settle(last)
                nc.vector.tensor_scalar(std[:, t0:t1], meanvar[:, t0:t1, 1], EPS, None, ALU.add).then_inc(var_ready, 1)

            def inverses(n, t0, t1):
                dve.wait_ge(std_ready, n)
                settle(nc.vector.reciprocal(rstd[:, t0:t1], std[:, t0:t1]))

            def norm(t0, t1):
                for t in range(t0, t1):
                    nc.vector.tensor_scalar(xn[:, t, :], xn[:, t, :], meanvar[:, t, 0:1], rstd[:, t:t + 1],
                                            ALU.subtract, ALU.mult).then_inc(normed_x, 1)

            def modulate(i):
                b, c = divmod(i, C)
                dve.wait_ge(ln_turned, i + 1)
                reach(dve, h_lo, max(i - 3, C) if i > 3 else 0)
                bank = 4 + i % 2 if i < 2 * C else 7
                nc.vector.tensor_scalar(h_f[:, i % 4], PS[:, bank], mod[:, CA * C + c, b:b + 1],
                                        mod[:, SA * C + c, b:b + 1], ALU.mult, ALU.add).then_inc(h_ready, 1)

            def batch_stats(b):
                dve.wait_ge(ld_x[b], 16)
                for t in range(b * TB, (b + 1) * TB):
                    last = measure(t, xn[:, t, :])
                return last

            settle(batch_stats(0))
            variances(0, TB)
            inverses(1, 0, TB)
            norm(0, TB)
            dve.wait_ge(mod_done, 1)
            settle(nc.vector.tensor_copy(mod[:, 0:2 * C, :], Op[:, 0:2 * C * B].rearrange("p (q b) -> p q b", b=B)))
            nc.vector.tensor_scalar(mod[:, CA * C:(CA + 1) * C, :], mod[:, CA * C:(CA + 1) * C, :], 1.0, None,
                                    ALU.add).then_inc(mod_ready, 1)
            dve.wait_ge(mod_ready, 1)
            settle(batch_stats(1))
            for i in range(C):
                modulate(i)
            batch_stats(2)
            dve.wait_ge(h_hi, 2)
            dve.wait_ge(h_lo, 1)
            nc.vector.tensor_tensor(hT_lo[:, 1, cols(0)], h_f[:, 1], hT_hi[:, 1, cols(0)].bitcast(F32),
                                    ALU.subtract).then_inc(h_lo, 1)
            variances(TB, 2 * TB)
            inverses(2, TB, 2 * TB)
            norm(TB, 2 * TB)

            def rope_cos(h, s, k):
                dve.wait_ge(qk_done, h * 2 + (k + 1))
                reach(dve, rotated, h * 2 + (k - 1) if not isinstance(h, int) or h > 0 else 0)
                nc.vector.tensor_tensor(cosx[:, k], QKp[:, k], rope_sb[:, k], ALU.mult)

            def rope_sin(h, s, k):
                nc.vector.tensor_tensor(sinx[0:64, k], QKp[64:128, k], rope_sb[64:128, 2 + k], ALU.mult)
                nc.vector.tensor_tensor(sinx[64:128, k], QKp[0:64, k], rope_sb[0:64, 2 + k],
                                        ALU.mult).then_inc(roped, 1)

            def out_low(h, s):
                dve.wait_ge(ao_hi_done, h + 1)
                u, j = (s // 2) % 2, s % 2
                nc.vector.tensor_tensor(ao_lo[:, u, j, :], Op, ao_hi[:, u, j, :].bitcast(F32),
                                        ALU.subtract).then_inc(ao_lo_done, 1)

            def add_y(y, s):
                b, c = (s // 2) % B, s % 2
                dve.wait_ge(projected, y + (1 + Y_CREDIT))
                nc.vector.scalar_tensor_tensor(accT[:, c, cols(b)], VYp, gate[:, 0, c, b:b + 1], accT[:, c, cols(b)],
                                               ALU.mult, ALU.add).then_inc(added, 1)

            def measure_x1(u):
                dve.wait_ge(x1_turned, u + 1)
                for t in range(2 * u, 2 * u + 2):
                    last = measure(t, PS[:, x1_bank(u), (t % 2) * M:(t % 2 + 1) * M])
                last.then_inc(x1_measured, 1)

            def head(base, s, last_heads=False):
                m = base + s
                par = s % 2
                steady = not isinstance(m, int)

                def row_max(o):
                    w = (QB[o] + 1) * P
                    dve.wait_ge(scored, m * 4 + (o + 1))
                    dve.nop(nofuse=True)
                    nc.vector.tensor_tensor_reduce(Sp[:, o % 2, 0:w], Sp[:, o % 2, 0:w], mask[:, T - w:T], -1.0, 3e38,
                                                   ALU.add, ALU.min, negmax[:, par, o:o + 1]).then_inc(maxed, 1)

                def scale(o):
                    qb = QB[o]
                    w = (qb + 1) * P
                    dve.wait_ge(exped, m * 4 + (o + 1))
                    nc.vector.reciprocal(rinv[:, par, o:o + 1], rowsum[:, par, o:o + 1]).then_inc(inverted, 1)
                    dve.wait_ge(inverted, m * 4 + (o + 1))
                    nc.vector.tensor_scalar(prob[:, qb, 0:w], prob[:, qb, 0:w], rinv[:, par, o:o + 1], None,
                                            ALU.mult).then_inc(scaled, 1)

                more = not last_heads or s < HEADS - 1
                first_norm = isinstance(m, int) and m in (1, 2)
                row_max(0)
                row_max(1)
                if last_heads and s == HEADS - 1:
                    measure_x1(2)
                if first_norm:
                    modulate((m + 1) * C)
                if not isinstance(m, int) or m >= 3:
                    add_y(m - 3, s - 3)
                scale(0)
                if not steady:
                    row_max(2)
                if first_norm:
                    modulate((m + 1) * C + 1)
                if isinstance(m, int) and m == 1:
                    norm(3 * TB, NT)
                if last_heads and s == HEADS - 2:
                    measure_x1(0)
                if last_heads and s == HEADS - 1:
                    measure_x1(3)
                if more:
                    rope_cos(m + 1, s + 1, 1)
                    rope_sin(m + 1, s + 1, 1)
                scale(1)
                if steady:
                    row_max(2)
                    out_low(m - 1, s - 1)
                scale(2)
                if last_heads and s == HEADS - 1:
                    dve.wait_ge(x1_measured, NT // 4)
                    variances(0, NT // 2)
                row_max(3)
                if not steady and m >= 1:
                    out_low(m - 1, s - 1)
                scale(3)
                if last_heads and s == HEADS - 2:
                    measure_x1(1)
                if not last_heads or s < HEADS - 2:
                    rope_cos(m + 2, s + 2, 0)
                    rope_sin(m + 2, s + 2, 0)

            dve.sem_inc(added, ADD_CREDIT)
            dve.wait_ge(ld_rope, 16)
            for k in range(2):
                rope_cos(0, 0, k)
                rope_sin(0, 0, k)
            for i in range(C, 2 * C):
                modulate(i)
            rope_cos(1, 1, 0)
            rope_sin(1, 1, 0)
            settle(batch_stats(3))
            variances(2 * TB, NT)
            dve.wait_ge(ld_mask, 32)
            head(0, 0)
            inverses(3, 2 * TB, NT)
            norm(2 * TB, 3 * TB)
            dve.wait_ge(mod_done, 2)
            nc.vector.tensor_copy(mod[:, 2 * C:6 * C, :],
                                         Op[:, 2 * C * B:6 * C * B].rearrange("p (q b) -> p q b", b=B)).then_inc(mod_ready, 1)
            for m in range(1, FIRST):
                head(0, m)
            dve.wait_ge(mod_ready, 2)
            nc.vector.tensor_scalar(mod[:, CB * C:(CB + 1) * C, :], mod[:, CB * C:(CB + 1) * C, :], 1.0, None, ALU.add)
            for n, s in enumerate((GA, GB)):
                g = mod[:, s * C:(s + 1) * C, :]
                nc.vector.tensor_scalar(gsign[:, n], g, 0.0, 2.0, ALU.is_ge, ALU.mult)
                last = nc.vector.tensor_scalar(gabs[:, n], g, -1.0, None, ALU.mult)
            settle(last)
            settle(nc.vector.tensor_scalar(gsign[:, :], gsign[:, :], -1.0, None, ALU.add))
            for n, s in enumerate((GA, GB)):
                last = nc.vector.tensor_tensor(gabs[:, n], gabs[:, n], mod[:, s * C:(s + 1) * C, :], ALU.max)
            settle(last)
            settle(nc.vector.tensor_scalar(gabs[:, :], gabs[:, :], 0.25, None, ALU.max))
            nc.vector.tensor_tensor(gate[:, :], gabs[:, :], gsign[:, :], ALU.mult).then_inc(mod_ready, 1)
            dve.wait_ge(mod_ready, 3)
            dve.wait_ge(ld_acc, 16)
            with dve.Fori(0, LOOPS) as p:
                for s in range(FIRST, FIRST + PER_PAIR):
                    head(p * PER_PAIR, s)
            for s in range(FIRST + LOOPS * PER_PAIR, HEADS):
                head(0, s, last_heads=True)
            add_y(HEADS - 3, HEADS - 3)
            inverses(4, 0, NT // 2)
            dve.wait_ge(x1_copied, NT // 4)
            norm(0, NT // 2)
            out_low(HEADS - 1, HEADS - 1)
            add_y(HEADS - 2, HEADS - 2)
            measure_x1(4)
            measure_x1(5)
            add_y(HEADS - 1, HEADS - 1)

            def router_shift(half):
                dve.wait_ge(logits_done, half + 1)
                t = slice(half * NT // 2, (half + 1) * NT // 2)
                lg = PS[:, 5, 0:NT // 2 * E].rearrange("p (i e) -> p i e", e=E)
                settle(nc.vector.tensor_reduce(lmax[:, t], lg, AX.X, ALU.max))
                nc.vector.tensor_tensor(logit[:, t, :], lg, lmax[:, t].unsqueeze(2).to_broadcast([P, NT // 2, E]),
                                        ALU.subtract).then_inc(shifted, 1)

            def router_top(half):
                dve.wait_ge(ex_done, half + 1)
                t = slice(half * NT // 2, (half + 1) * NT // 2)
                for i in range(half * NT // 2, (half + 1) * NT // 2):
                    last = nc.vector.max(top[:, i, :], ex[:, i, :])
                settle(last)
                for i in range(half * NT // 2, (half + 1) * NT // 2):
                    last = nc.vector.match_replace(out=rest[:, i, :], in_to_replace=top[:, i, :],
                                                   in_values=ex[:, i, :], imm_value=0.0)
                settle(last)
                settle(nc.vector.tensor_tensor(w_f[:, t, :], ex[:, t, :], rest[:, t, :], ALU.subtract))
                settle(nc.vector.tensor_reduce(wsum[:, t], w_f[:, t, :], AX.X, ALU.add))
                settle(nc.vector.reciprocal(winv[:, t], wsum[:, t]))

            def router_weights(half):
                t = slice(half * NT // 2, (half + 1) * NT // 2)
                settle(nc.vector.tensor_tensor(w_f[:, t, :], w_f[:, t, :],
                                               winv[:, t].unsqueeze(2).to_broadcast([P, NT // 2, E]), ALU.mult))
                settle(nc.vector.tensor_copy(w_b[:, t, 0, :], w_f[:, t, :]))
                settle(nc.vector.tensor_tensor(w_r[:, t, :], w_f[:, t, :], w_b[:, t, 0, :], ALU.subtract))
                settle(nc.vector.tensor_copy(w_b[:, t, 1, :], w_r[:, t, :]))
                nc.vector.tensor_tensor(w_b[:, t, 2, :], w_r[:, t, :], w_b[:, t, 1, :],
                                        ALU.subtract).then_inc(w_split, 1)

            def router_out(half):
                dve.wait_ge(wT_done, half + 1)
                nc.vector.tensor_copy(wT_b[:, half * N // 2:(half + 1) * N // 2],
                                      PS[0:KS, 5, :].bitcast(BF16)).then_inc(wT_ready, 1)

            def times_weight(t, s, grp):
                dve.wait_ge(sil_done, t + 1)
                if s < FIRST_STEP:
                    dve.wait_ge(wb_done, t + 1)
                    weights = PS[:, 4 + s % 2]
                else:
                    j, b = place(s)
                    if b == 0:
                        dve.wait_ge(ld_w[j], grp * 32 + 32 * (s // PER_GROUP))
                    weights = w_ring[:, j, cols(b)]
                nc.vector.tensor_tensor(silw[:, s % 2], weights, sil[:, s % 2], ALU.mult).then_inc(silw_done, 1)

            def times_up(t, s):
                dve.wait_ge(u_done, t + 1)
                dve.wait_ge(silw_done, t + 1)
                dve.wait_ge(hv_lo_done, t - 1)
                nc.vector.tensor_tensor(hv[:, s % 2], PS[:, 2 + s % 2], silw[:, s % 2], ALU.mult).then_inc(hv_done, 1)

            def up_first(t):
                dve.wait_ge(sil_done, t + 1)
                dve.wait_ge(u_done, t + 1)
                nc.vector.tensor_tensor(h_f[:, t % 4], PS[:, 2 + t % 2], sil[:, t % 2], ALU.mult).then_inc(silw_done, 1)

            def weight_after(t):
                dve.wait_ge(silw_done, t + 1)
                dve.wait_ge(wb_done, t + 1)
                reach(dve, hv_lo_done, t - 1)
                nc.vector.tensor_tensor(hv[:, t % 2], PS[:, 4], h_f[:, t % 4], ALU.mult).then_inc(hv_done, 1)

            def add_down(t, s):
                b = place(s)[1]
                dve.wait_ge(down_done, t + 1)
                for c in range(C):
                    if isinstance(t, int) and t == STEPS - 1 and c > 0:
                        last.then_inc(y_added, 1)
                    last = nc.vector.scalar_tensor_tensor(accT[:, c, cols(b)], PS[:, 6 + c], gate[:, 1, c, b:b + 1],
                                                          accT[:, c, cols(b)], ALU.mult, ALU.add)
                last.then_inc(y_added, 1)

            def step(base, s, grp):
                t = base + s
                times_weight(t, s, grp)
                times_up(t, s)
                add_down(t - 1, s - 1)

            def finish(u):
                weight_after(u)
                if u > 0:
                    add_down(u - 1, u - 1)

            router_shift(0)
            measure_x1(6)
            measure_x1(7)
            dve.wait_ge(x1_measured, NT // 2)
            variances(NT // 2, NT)
            router_top(0)
            up_first(0)
            router_weights(0)
            up_first(1)
            router_out(0)
            for t in range(2, PER_GROUP):
                if t == 9:
                    router_out(1)
                if t == 6:
                    router_shift(1)
                if t in AFTER_GATE:
                    finish(AFTER_GATE[t])
                up_first(t)
                if t in AFTER_UP:
                    finish(AFTER_UP[t])
                if t == 3:
                    inverses(5, NT // 2, NT)
                    dve.wait_ge(x1_copied, NT // 2)
                    norm(NT // 2, NT - TB)
                if t == 4:
                    norm(NT - TB, NT)
                if t == 6:
                    router_top(1)
                if t == 7:
                    router_weights(1)
            for t in range(PER_GROUP, FIRST_STEP):
                step(0, t, 0)
            dve.wait_ge(ld_w[0], 32)
            with dve.Fori(0, GROUPS - 2) as g:
                for s in range(FIRST_STEP, FIRST_STEP + PER_GROUP):
                    step(g * PER_GROUP, s, g)
            for t in range(FIRST_STEP + (GROUPS - 2) * PER_GROUP, STEPS):
                step(0, t, 0)
            add_down(STEPS - 1, STEPS - 1)

        @block.gpsimd
        def _(pool):
            def low(dst, src, hi):
                return nc.gpsimd.tensor_tensor(dst, src, hi.bitcast(F32), ALU.subtract)

            def low_qk(j, n):
                pool.wait_ge(whi_qk, n)
                low(qk_lo[:, j], raw_qk[:, j], qk_hi[:, j]).then_inc(wlo_qk, 1)

            def low_v(n):
                pool.wait_ge(whi_v, n)
                low(v_lo[:, :, :], raw_v[:, :, :], v_hi[:, :, :]).then_inc(wlo_v, 1)

            def low_o(n):
                pool.wait_ge(whi_o, n)
                low(o_lo[:, :, :], raw_o[:, :, :], o_hi[:, :, :]).then_inc(wlo_o, 1)

            def h_low(b, r=0):
                for c in range(C):
                    i = b * C + c
                    pool.wait_ge(h_hi, B * C * r + i + 1)
                    src = h_f[:, i % 4] if r == 0 else h2_f[:, c, cols(b)]
                    low(hT_lo[:, c, cols(b)], src, hT_hi[:, c, cols(b)]).then_inc(h_lo, 1)

            low_qk(0, 1)
            pool.wait_ge(h_hi, 1)
            low(hT_lo[:, 0, cols(0)], h_f[:, 0], hT_hi[:, 0, cols(0)]).then_inc(h_lo, 1)
            low_v(1)

            def rotate_add(h, k):
                pool.wait_ge(roped, h * 2 + (k + 1))
                nc.gpsimd.tensor_tensor(rot_f[:, k], cosx[:, k], sinx[:, k], ALU.add).then_inc(rotated, 1)

            def rotate_low(h, s, k):
                pool.wait_ge(rot_hi_done, h * 2 + (k + 1))
                low(rot_lo[:, s % 2, k], rot_f[:, k], rot_hi[:, s % 2, k]).then_inc(rot_lo_done, 1)

            def rotate(h, s, k):
                rotate_add(h, k)
                rotate_low(h, s, k)

            def head(base, s, pair, last_heads=False):
                m = base + s
                nl = s // PER_PAIR
                r = s % PER_PAIR
                if r == 2:
                    low_o(pair + (nl + 1))
                if not last_heads or s < HEADS - 1:
                    rotate(m + 1, s + 1, 1)
                if isinstance(m, int) and m in (1, 2):
                    h_low(m + 1)
                if not last_heads or s < HEADS - 2:
                    rotate_add(m + 2, 0)
                    if r == 5 and not last_heads:
                        low_v(pair + (nl + 2))
                    if r == 6 and not last_heads:
                        low_qk(1, pair * 2 + (2 * nl + 4))
                    rotate_low(m + 2, s + 2, 0)
                    if r == 5 and not last_heads:
                        low_qk(0, pair * 2 + (2 * nl + 3))

            low_qk(1, 2)
            for k in range(2):
                rotate_add(0, k)
            for k in range(2):
                rotate_low(0, 0, k)
            h_low(1)
            pool.wait_ge(rot_lo_done, 1)
            rotate(1, 1, 0)
            for m in range(FIRST):
                head(0, m, 0)
            with pool.Fori(0, LOOPS) as p:
                for s in range(FIRST, FIRST + PER_PAIR):
                    head(p * PER_PAIR, s, p)
            for s in range(FIRST + LOOPS * PER_PAIR, HEADS):
                head(0, s, 0, last_heads=True)

            def low_e(j, n):
                pool.wait_ge(whi_e, n)
                low(gu_lo[:, j], raw_gu[:, j], gu_hi[:, j])
                low(d_lo[:, j], raw_d[:, j], d_hi[:, j]).then_inc(wlo_e, 1)

            def hv_low(t, s):
                pool.wait_ge(hv_hi_done, t + 1)
                low(hv_lo[:, s % 2], hv[:, s % 2], hv_hi[:, s % 2]).then_inc(hv_lo_done, 1)

            def step(base, s, grp, end=False):
                t = base + s
                hv_low(t, s)
                q = s // B + 2
                if s % B == 1 and not (end and q >= CH):
                    low_e(q % GROUP, grp * GROUP + (q + 1))

            for q in range(GROUP):
                low_e(q, q + 1)
            h_low(0, 1)
            h_low(1, 1)
            for t in range(PER_GROUP):
                if t in (5, 6):
                    h_low(t - 3, 1)
                if t in AFTER_GATE:
                    hv_low(AFTER_GATE[t], AFTER_GATE[t])
                if t == 11:
                    low_e(0, 4)
                if t in AFTER_UP:
                    hv_low(AFTER_UP[t], AFTER_UP[t])
            low_e(1, 5)
            for t in range(PER_GROUP, FIRST_STEP):
                step(0, t, 0)
            with pool.Fori(0, GROUPS - 2) as g:
                for s in range(FIRST_STEP, FIRST_STEP + PER_GROUP):
                    step(g * PER_GROUP, s, g)
            for t in range(FIRST_STEP + (GROUPS - 2) * PER_GROUP, STEPS):
                step(0, t, 0, end=True)


def kernel(L0_attn_x, L0_attn_wq, L0_attn_wk, L0_attn_wv, L0_attn_wo, L0_ffn_router_w,
           L0_ffn_w_gate, L0_ffn_w_up, L0_ffn_w_down, L0_c, L0_wmod):
    import concourse.bacc as bacc
    from concourse.bass_utils import run_bass_kernel_spmd

    a = [np.asarray(v) for v in (L0_attn_x, L0_attn_wq, L0_attn_wk, L0_attn_wv, L0_attn_wo, L0_ffn_router_w,
                                 L0_ffn_w_gate, L0_ffn_w_up, L0_ffn_w_down, L0_c, L0_wmod)]
    x, wq, wk, wv, wo, rw, wg, wu, wd, c, wmod = a
    flat = x.reshape(N, M)

    def halves(w):
        return w.reshape(C, P, -1).transpose(1, 0, 2)

    half = D // 2
    freqs = np.power(np.float32(10000.0), -(np.arange(half, dtype=np.float32) / np.float32(half)))
    rad = np.arange(T, dtype=np.float32)[:, None] * freqs[None, :]
    cos, sin = np.cos(rad).T, np.sin(rad).T
    cos2, sin2 = np.concatenate([cos, cos]), np.concatenate([sin, -sin])
    scale = np.float32(1.0 / D)
    bf = mybir.dt.np(BF16)
    q_i, k_i = np.arange(P)[:, None], np.arange(P)[None, :]
    qk = np.stack([wq, wk], 0).reshape(2, C, P, PAIRS, 2, D)
    gu = np.stack([wg, wu], 0).transpose(0, 2, 1, 3).reshape(2, C, P, CH, P)
    arrays = {
        "x": flat.reshape(NT, P, M).transpose(1, 0, 2),
        "xT": flat.T.reshape(C, P, N).transpose(1, 0, 2),
        "cT": halves(c.T),
        "wmod": halves(wmod),
        "rwT": halves(rw.T),
        "rope": np.stack([cos2 * scale, cos2, sin2 * scale, sin2], 1),
        "ident": np.eye(P, dtype=np.float32),
        "identb": np.eye(P).astype(bf),
        "maskf": np.concatenate([np.zeros((P, T - P)), np.where(q_i < k_i, -1e30, 0.0)], 1).astype(np.float32),
        "selb": np.tile(np.repeat(np.eye(E), I, axis=1), (3, 1)).astype(bf),
        "wqk": qk.transpose(3, 4, 2, 1, 0, 5),
        "wv": wv.reshape(C, P, PAIRS, 2 * D).transpose(2, 1, 0, 3),
        "wo": wo.reshape(PAIRS, 2, D, M).transpose(0, 2, 1, 3),
        "wgu": gu.transpose(3, 2, 1, 0, 4),
        "wd": wd.reshape(CH, P, M),
    }
    nc = bacc.Bacc("TRN2", target_bir_lowering=False, num_devices=1)
    arrays = {k: np.ascontiguousarray(v) for k, v in arrays.items()}
    aps = [nc.dram_tensor(k, v.shape, mybir.dt.from_np(v.dtype), kind="ExternalInput").ap() for k, v in arrays.items()]
    outT = nc.dram_tensor("outT", (P, C, N), F32, kind="ExternalOutput").ap()
    w_dram = nc.dram_tensor("w_dram", (E, N), F32, kind="Internal").ap()
    build(nc, *aps, w_dram, outT)
    r = run_bass_kernel_spmd(nc, [arrays], core_ids=[0])
    y = r.results[0]["outT"]
    return np.ascontiguousarray(y.transpose(2, 1, 0)).reshape(B, T, M)
```
